# Optimizing a Trainium2 kernel written in Bass

```python
import numpy as np
import jax
import jax.numpy as jnp

def _softmax(x, axis=-1):
    return jax.nn.softmax(x, axis=axis)

def _gelu(x):
    return jax.nn.gelu(x, approximate=True)

def _silu(x):
    return jax.nn.silu(x)

def _sigmoid(x):
    return jax.nn.sigmoid(x)

def _layernorm(x, axis=-1, eps=1e-05):
    m = jnp.mean(x, axis=axis, keepdims=True)
    v = jnp.var(x, axis=axis, keepdims=True)
    return (x - m) / jnp.sqrt(v + eps)

def _scatter_add(tgt, idx, src, axis=0):
    return tgt.at[idx].add(src)

def _segment_sum(src, seg, n):
    return jax.ops.segment_sum(src, seg, n)
kernel_name = 'mk_gnn_resnorm_d1_gnn_r8_9a40d8'

def setup_inputs(seed: int=0):
    np.random.seed(seed)
    _w = jnp.asarray

    def _rec_inputs():
        import jax
        import jax.numpy as jnp
        _gk = jax.random.key(seed)
        x = -0.0004942 + 1 * jax.random.normal(jax.random.fold_in(_gk, 1), (6250, 128), jnp.float32)
        src = jax.random.randint(jax.random.fold_in(_gk, 2), (100000,), 0, 6250, jnp.int32)
        dst = jax.random.randint(jax.random.fold_in(_gk, 3), (100000,), 0, 6250, jnp.int32)
        _o = jnp.argsort(dst, stable=True)
        src = src[_o]
        dst = dst[_o]
        edge_type_6 = jax.random.randint(jax.random.fold_in(_gk, 12), (100000,), 0, 6, jnp.int32)
        node_type_3 = jax.random.randint(jax.random.fold_in(_gk, 13), (6250,), 0, 3, jnp.int32)
        return (x, src, dst, edge_type_6, node_type_3)
    x, src, dst, edge_type_6, node_type_3 = _rec_inputs()

    def _L0_gnn_setup():
        import jax, jax.numpy as jnp
        import numpy as np
        N, E, D_IN, H, HD = (3750, 30000, 128, 4, 32)
        NT, ET, L = (3, 6, 5)
        D = H * HD

        def typed_linear(x, types, W):
            out = jnp.zeros((x.shape[0], W.shape[-1]), x.dtype)
            for t in range(W.shape[0]):
                out = out + jnp.where((types == t)[:, None], x @ W[t], jnp.float32(0.0))
            return out

        def typed_linear_heads(xe, types, W):
            out = jnp.zeros(xe.shape, xe.dtype)
            for t in range(W.shape[1]):
                yt = jnp.einsum('ehd,hdo->eho', xe, W[:, t])
                out = out + jnp.where((types == t)[:, None, None], yt, jnp.float32(0.0))
            return out

        def hgt_conv(x, src, dst, ntype, etype, Wk, Wq, Wv, Wa, pri, att, msg, skip):
            n = x.shape[0]
            k = typed_linear(x, ntype, Wk).reshape(n, H, HD)
            q = typed_linear(x, ntype, Wq).reshape(n, H, HD)
            v = typed_linear(x, ntype, Wv).reshape(n, H, HD)
            kw = typed_linear_heads(k[src], etype, att)
            a = jnp.sum(kw * q[dst], axis=-1) * pri[:, etype].T / np.float32(np.sqrt(HD))
            amax = jax.ops.segment_max(a, dst, num_segments=n)
            amax = jnp.where(jnp.isfinite(amax), amax, jnp.float32(0.0))
            ae = jnp.exp(a - amax[dst])
            w = ae / jax.ops.segment_sum(ae, dst, num_segments=n)[dst]
            m = typed_linear_heads(v[src], etype, msg) * w[:, :, None]
            h = jax.ops.segment_sum(m, dst, num_segments=n).reshape(n, D)
            h = typed_linear(h, ntype, Wa)
            alpha = jax.nn.sigmoid(skip)[ntype][:, None]
            return h * alpha + x * (jnp.float32(1.0) - alpha)
        key = jax.random.key(seed)
        ks = jax.random.split(key, 12)
        s_in = np.float32(1.0 / np.sqrt(D_IN))
        s_d = np.float32(1.0 / np.sqrt(D))
        s_hd = np.float32(1.0 / np.sqrt(HD))
        return dict(x=jax.random.normal(ks[0], (N, D_IN), jnp.float32), Wk=jax.random.normal(ks[1], (L, NT, D_IN, D), jnp.float32) * s_in, Wq=jax.random.normal(ks[2], (L, NT, D_IN, D), jnp.float32) * s_in, Wv=jax.random.normal(ks[3], (L, NT, D_IN, D), jnp.float32) * s_in, Wa=jax.random.normal(ks[4], (L, NT, D, D), jnp.float32) * s_d, rel_pri=jnp.ones((L, H, ET), jnp.float32), rel_att=jax.random.normal(ks[5], (L, H, ET, HD, HD), jnp.float32) * s_hd, rel_msg=jax.random.normal(ks[6], (L, H, ET, HD, HD), jnp.float32) * s_hd, skip=jnp.ones((L, NT), jnp.float32), src=jax.random.randint(ks[7], (E,), 0, N, jnp.int32), dst=jax.random.randint(ks[8], (E,), 0, N, jnp.int32), ntype=jax.random.randint(ks[9], (N,), 0, NT, jnp.int32), etype=jax.random.randint(ks[10], (E,), 0, ET, jnp.int32))
    _L0_gnn_all = _L0_gnn_setup()
    _L0_gnn_in = {k: v for k, v in _L0_gnn_all.items() if k in ('Wk', 'Wq', 'Wv', 'Wa', 'rel_pri', 'rel_att', 'rel_msg', 'skip')}
    del _L0_gnn_all
    return {'x': x, 'src': src, 'dst': dst, 'edge_type_6': edge_type_6, 'node_type_3': node_type_3, 'L0_gnn_Wk': _L0_gnn_in['Wk'], 'L0_gnn_Wq': _L0_gnn_in['Wq'], 'L0_gnn_Wv': _L0_gnn_in['Wv'], 'L0_gnn_Wa': _L0_gnn_in['Wa'], 'L0_gnn_rel_pri': _L0_gnn_in['rel_pri'], 'L0_gnn_rel_att': _L0_gnn_in['rel_att'], 'L0_gnn_rel_msg': _L0_gnn_in['rel_msg'], 'L0_gnn_skip': _L0_gnn_in['skip']}

def reference(x, src, dst, edge_type_6, node_type_3, L0_gnn_Wk, L0_gnn_Wq, L0_gnn_Wv, L0_gnn_Wa, L0_gnn_rel_pri, L0_gnn_rel_att, L0_gnn_rel_msg, L0_gnn_skip):
    import jax
    import jax.numpy as jnp

    def _L0_gnn_ref(x, Wk, Wq, Wv, Wa, rel_pri, rel_att, rel_msg, skip, src, dst, ntype, etype):
        import jax, jax.numpy as jnp
        import numpy as np
        N, E, D_IN, H, HD = (3750, 30000, 128, 4, 32)
        NT, ET, L = (3, 6, 5)
        D = H * HD

        def typed_linear(x, types, W):
            out = jnp.zeros((x.shape[0], W.shape[-1]), x.dtype)
            for t in range(W.shape[0]):
                out = out + jnp.where((types == t)[:, None], x @ W[t], jnp.float32(0.0))
            return out

        def typed_linear_heads(xe, types, W):
            out = jnp.zeros(xe.shape, xe.dtype)
            for t in range(W.shape[1]):
                yt = jnp.einsum('ehd,hdo->eho', xe, W[:, t])
                out = out + jnp.where((types == t)[:, None, None], yt, jnp.float32(0.0))
            return out

        def hgt_conv(x, src, dst, ntype, etype, Wk, Wq, Wv, Wa, pri, att, msg, skip):
            n = x.shape[0]
            k = typed_linear(x, ntype, Wk).reshape(n, H, HD)
            q = typed_linear(x, ntype, Wq).reshape(n, H, HD)
            v = typed_linear(x, ntype, Wv).reshape(n, H, HD)
            kw = typed_linear_heads(k[src], etype, att)
            a = jnp.sum(kw * q[dst], axis=-1) * pri[:, etype].T / np.float32(np.sqrt(HD))
            amax = jax.ops.segment_max(a, dst, num_segments=n)
            amax = jnp.where(jnp.isfinite(amax), amax, jnp.float32(0.0))
            ae = jnp.exp(a - amax[dst])
            w = ae / jax.ops.segment_sum(ae, dst, num_segments=n)[dst]
            m = typed_linear_heads(v[src], etype, msg) * w[:, :, None]
            h = jax.ops.segment_sum(m, dst, num_segments=n).reshape(n, D)
            h = typed_linear(h, ntype, Wa)
            alpha = jax.nn.sigmoid(skip)[ntype][:, None]
            return h * alpha + x * (jnp.float32(1.0) - alpha)
        h = x
        for l in range(L):
            h = hgt_conv(h, src, dst, ntype, etype, Wk[l], Wq[l], Wv[l], Wa[l], rel_pri[l], rel_att[l], rel_msg[l], skip[l])
        return h
    x = _layernorm(x + _L0_gnn_ref(x, L0_gnn_Wk, L0_gnn_Wq, L0_gnn_Wv, L0_gnn_Wa, L0_gnn_rel_pri, L0_gnn_rel_att, L0_gnn_rel_msg, L0_gnn_skip, src, dst, node_type_3, edge_type_6), axis=-1)
    return x

_drawn_inputs = setup_inputs


def setup_inputs(seed=0):
    import zlib

    import numpy as np

    out = dict(_drawn_inputs(seed))
    spreads = {'L0_gnn_rel_pri': (1.0, 0.6), 'L0_gnn_skip': (1.0, 0.6)}
    factors = {'L0_gnn_Wk': 8.0,
     'L0_gnn_Wq': 8.0,
     'L0_gnn_Wv': 8.0,
     'L0_gnn_Wa': 8.0,
     'L0_gnn_rel_att': 8.0,
     'L0_gnn_rel_msg': 8.0}
    for name, (base, spread) in spreads.items():
        noise = np.random.default_rng([zlib.crc32(name.encode()), seed]).standard_normal(out[name].shape)
        drawn = base * np.exp(spread * noise) if base else spread * noise
        out[name] = jnp.asarray(drawn.astype(out[name].dtype))
    for name, factor in factors.items():
        out[name] = (out[name] * factor).astype(out[name].dtype)
    return out
```

```python
from contextlib import ExitStack

import concourse.bass as bass
from concourse import mybir

F32 = mybir.dt.float32
BF16 = mybir.dt.bfloat16
I32 = mybir.dt.int32
ALU = mybir.AluOpType
ACT = mybir.ActivationFunctionType
AX = mybir.AxisListType.X

P = 128
N, E, D, H, HD = 6250, 100000, 128, 4, 32
NT, ET, L = 3, 6, 5
TILES = -(-N // P)
LAST = N - (TILES - 1) * P
CHUNKS = -(-E // P)
CB = -(-CHUNKS // P)
STEPS = CHUNKS + TILES - 1
QUADS = -(-STEPS // 4)
SB = -(-4 * QUADS // P)
SP_ = SB * P
HALF = 8
ITERS = (QUADS - 2 * HALF) // (2 * HALF)
assert QUADS == 2 * HALF + ITERS * 2 * HALF
TU = 8
TN = 13
TNS = -(-TILES // TN)
TITERS = (TILES - 1 - 2 * TU) // TU
assert TILES == 2 * TU + TITERS * TU + 1
ROW = 2 * D
AW = D + H
BIG = 1.5e38
NO_DST = 30000.0
EPS = 1e-5
R4 = D // 32


def gnn(nc, x, src, dst, etype, ntype, Wk, Wq, Wv, Wa, pri, att, msg, skip, out):
    table = nc.dram_tensor("table", (TILES * P * ET, ROW), F32, kind="Internal").ap()
    table_tiles = table.rearrange("(t p e) c -> t p (e c)", p=P, e=ET)
    messages = nc.dram_tensor("messages", (QUADS, P, 4 * D), F32, kind="Internal").ap()

    with ExitStack() as ctx:
        def sb(name, shape, dt=F32):
            return ctx.enter_context(nc.sbuf_tensor(name, shape, dt))

        def sem(name):
            return ctx.enter_context(nc.semaphore(name))

        ps = ctx.enter_context(nc.psum_tensor("ps", [P, 8, 512], F32))
        psf = ps[:].rearrange("p b c -> p (b c)")

        ident = sb("ident", [P, P])
        identb = sb("identb", [P, P], BF16)
        iota_n = sb("iota_n", [P, P])
        iota_nb = sb("iota_nb", [P, P], BF16)
        iota_p = sb("iota_p", [P, 1])
        ones = sb("ones", [P, P])
        pick = sb("pick", [P, 2, 4])
        idx = sb("idx", [P, SP_], I32)
        dloc = sb("dloc", [P, SP_])
        tile_of = sb("tile_of", [1, SP_], I32)
        idx_now = sb("idx_now", [P, 2, 4 * HALF], I32)
        seg_cap = sb("seg_cap", [P, SB * H * P + 1], BF16)
        lane_cap = sb("lane_cap", [P, SB, P], BF16)
        join = sb("join", [H, SP_ + 1], BF16)
        join_fwd = sb("join_fwd", [H, SP_], BF16)
        join_bwd = sb("join_bwd", [H, SP_], BF16)
        tmask = sb("tmask", [P, TILES, NT])
        alpha = sb("alpha", [P, L, TILES])
        beta = sb("beta", [P, L, TILES])
        wk = sb("wk", [P, NT, D])
        wq = sb("wq", [P, NT, D])
        wv = sb("wv", [P, NT, D])
        wa = sb("wa", [P, NT, D])
        attw = sb("attw", [P, ET, D])
        msgw = sb("msgw", [P, ET, D])
        priw = sb("priw", [P, H, ET])
        h = sb("h", [P, TILES, D])
        node = sb("node", [P, TILES, AW])
        score = sb("score", [P, SP_, H])
        aT = sb("aT", [P, SB, H, P])
        mT = sb("mT", [P, SB, H, P])
        rows = sb("rows", [P, HALF, 4, ROW])
        oh = sb("oh", [P, 4, 4, P], BF16)
        ohT = sb("ohT", [P, 2, 4, P])
        prod = sb("prod", [P, 2, 4 * D])
        wmsg = sb("wmsg", [P, 2, 4, AW])

        flat = rows[:].rearrange("p a b c -> p (a b c)")
        off = [0]

        def carve(*shape):
            n = 1
            for v in shape:
                n *= v
            v = flat[:, off[0]:off[0] + n]
            off[0] += n
            assert off[0] <= HALF * 4 * ROW
            return v
        tab = carve(2, ET * ROW).rearrange("p (b e c) -> p b e c", b=2, e=ET)
        hm = carve(2, NT * D).rearrange("p (b t c) -> p b t c", b=2, t=NT)
        hmT = carve(2, NT * D).rearrange("p (b t c) -> p b t c", b=2, t=NT)
        kvT = carve(2, 2 * D).rearrange("p (b t c) -> p b t c", b=2, t=2)
        rden = carve(TILES, H).rearrange("p (t c) -> p t c", c=H)
        run_f = flat[0:H, 0:SP_ + 1]
        run_b = flat[0:H, 1024:1024 + SP_ + 1]
        carry = flat[0:H, 2048:2048 + 2 * SP_].rearrange("p (b s) -> p b s", b=2)
        mbuf = flat[:, 0:HALF * 4 * D].rearrange("p (q c) -> p q c", q=HALF)

        s_load = sem("graph_loaded")
        s_x = sem("x_loaded")
        s_pool0 = sem("constants_ready")
        s_pre = sem("prepare_dve")
        s_prepe = sem("prepare_pe")
        s_w = sem("weights_loaded")
        s_wa = sem("wa_loaded")
        s_phase = sem("phase_ends")
        s_held = sem("waits_held")
        s_hm = sem("masked_ready")
        s_tr = sem("transposed")
        s_hmT = sem("masked_transposed")
        s_kvq = sem("kvq_done")
        s_kvT = sem("kv_copied")
        s_qn = sem("q_copied")
        s_tabp = sem("table_products")
        s_tabk = sem("table_k_half")
        s_tabv = sem("table_v_half")
        s_tabst = [sem(f"table_stored{i}") for i in range(2)]
        s_hn = sem("normalised")
        s_g = sem("wa_product")
        s_h = sem("h_updated")
        s_gath = [sem(f"gathered{i}") for i in range(HALF)]
        s_vst = [sem(f"messages_stored{i}") for i in range(HALF)]
        s_vld = [sem(f"messages_loaded{i}") for i in range(HALF)]
        s_oh = sem("onehot_ready")
        s_ohp = sem("onehot_transposed")
        s_ohT = sem("onehot_copied")
        s_qe = sem("q_expanded")
        s_dot = sem("dots_done")
        s_wm = sem("weighted_ready")
        s_ohf = sem("onehot32_ready")
        s_agg = sem("summed")
        s_add = sem("accumulated")
        s_smt = sem("scores_transposed")
        s_sml = sem("ends_transposed")
        s_smc = sem("carries_transposed")
        s_smd = sem("softmax_dve")
        s_sme = sem("exp_done")
        s_smb = sem("exp_transposed")
        s_act = sem("gates_and_roots")
        s_out = sem("out_stored")

        def quads(eng, body):
            for k in range(HALF):
                body(k, k, 0)
            with eng.Fori(0, ITERS) as it:
                for k in range(2 * HALF):
                    body(it * (2 * HALF) + (HALF + k), k % HALF, it * 2 + (1 + k // HALF))
            for k in range(HALF):
                body(QUADS - HALF + k, k, QUADS // HALF - 1)

        def tiles(eng, body):
            for k in range(TU):
                body(k, k % 2, k // 2)
            with eng.Fori(0, TITERS) as it:
                for k in range(TU):
                    body(it * TU + (TU + k), k % 2, it * (TU // 2) + (TU + k) // 2)
            for k in range(TILES - TU - 1, TILES):
                body(k, k % 2, k // 2)

        def stores_before(l, b, pair):
            return (l * (TILES - TILES // 2 if b == 0 else TILES // 2) + pair) * 16

        def at(i, n=1):
            return bass.ds(i, n)

        def tiles_of(q, engine):
            _, ts = nc.values_load_multi_w_load_instructions(
                tile_of[0:1, at(4 * q, 4)], engines=[engine], min_val=0, max_val=TILES - 1,
                skip_runtime_bounds_check_because="a step's tile counts the tiles 1..TILES-1 that began before it")
            return ts

        def is_first(v, n=1):
            return isinstance(v, int) and v < n

        def is_last(v, total):
            return isinstance(v, int) and v == total - 1

        def hold(eng, semaphore, value):
            eng.wait_ge(semaphore, value)
            eng.sem_inc(s_held, 1)

        def end_phase(eng, number):
            eng.drain().then_inc(s_phase, 1)
            hold(eng, s_phase, 5 * number)

        PER = 5

        def number(l, k):
            return 2 + l * PER + k

        def layers(eng, score_, softmax_, gatherup_, output_, project_, last=None):
            end_phase(eng, 1)
            project_(0, 0)
            end_phase(eng, 2)

            def one(l):
                score_(l)
                end_phase(eng, number(l, 1))
                softmax_(l)
                end_phase(eng, number(l, 2))
                gatherup_(l)
                end_phase(eng, number(l, 3))
                output_(l)
                end_phase(eng, number(l, 4))
            with eng.Fori(0, L - 1) as l:
                one(l)
                project_(l + 1, 1)
                end_phase(eng, number(l, 5))
            one(L - 1)
            if last:
                last()

        def tr_base(l, out_):
            return l * (2 * TILES) + (TILES if out_ else 0)

        SMD = 3

        def prep_arrays():
            a = aT[:].rearrange("p a b c -> p (a b c)")
            m = mT[:].rearrange("p a b c -> p (a b c)")
            n = CB * P
            return ((a[:, n:2 * n].rearrange("p (k c) -> p k c", k=CB), 0),
                    (m[:, n:2 * n].rearrange("p (k c) -> p k c", k=CB), 1))

        def prep_sel(kb):
            return flat[:, 1024 + kb * SP_:1024 + (kb + 1) * SP_]

        def prep_dst():
            return aT[:].rearrange("p a b c -> p (a b c)")[:, 2 * CB * P:2 * CB * P + SP_]

        block = ctx.enter_context(nc.Block())

        @block.sync
        def _(sp):
            full = (E // P) // P
            rest = E // P - full * P
            tail = E - (E // P) * P
            for a, b in ((dst, 0), (src, 1), (etype, 2)):
                v = (aT, mT, rows)[b][:].rearrange("p a b c -> p (a b c)")[:, 0:CB * P]
                v = v.bitcast(I32).rearrange("p (k c) -> p k c", k=CB)
                sp.wait_ge(s_pool0, 3)
                sp.dma_start(v[:, 0:full, :], a[0:full * P * P].rearrange("(k p c) -> p k c", p=P, c=P)
                             ).then_inc(s_load, 16)
                sp.dma_start(v[0:rest, full, :],
                             a[full * P * P:(full * P + rest) * P].rearrange("(p c) -> p c", c=P)
                             ).then_inc(s_load, 16)
                sp.dma_start(v[rest:rest + 1, full, 0:tail],
                             a[E - tail:E].rearrange("(p c) -> p c", p=1)).then_inc(s_load, 16)
            nt_raw = oh[:].rearrange("p a b c -> p (a b c)").bitcast(I32)[:, 0:TILES]
            sp.dma_start(nt_raw[:, 0:TILES - 1],
                         ntype[0:(TILES - 1) * P].rearrange("(t p) -> p t", p=P),
                         allow_slow_non_contiguous=True).then_inc(s_load, 16)
            sp.dma_start(nt_raw[0:LAST, TILES - 1:TILES],
                         ntype[(TILES - 1) * P:N].rearrange("(p t) -> p t", t=1)).then_inc(s_load, 16)
            sp.dma_start(alpha[:, :, 0:NT], skip.rearrange("(o l) t -> o l t", o=1).broadcast_to((P, L, NT))
                         ).then_inc(s_load, 16)
            sp.dma_start(h[:, 0:TILES - 1, :], x[0:(TILES - 1) * P, :].rearrange("(t p) c -> p t c", p=P)
                         ).then_inc(s_x, 16)
            sp.dma_start(h[0:LAST, TILES - 1, :], x[(TILES - 1) * P:N, :]).then_inc(s_x, 16)
            sp.wait_ge(s_x, 32)

            def weights(l):
                for w, d in ((wk, Wk), (wq, Wq), (wv, Wv)):
                    for r in range(R4):
                        sp.dma_start(w[32 * r:32 * r + 32, :, :],
                                     d[at(l), :, r:D:R4, :].rearrange("l t i o -> (l i) t o")).then_inc(s_w, 16)
                for w, d in ((attw, att), (msgw, msg)):
                    for hh in range(H):
                        a, b = HD * hh, HD * hh + HD
                        sp.dma_start(w[a:b, :, a:b],
                                     d[at(l), hh, :, :, :].rearrange("l t i o -> (l i) t o")).then_inc(s_w, 16)
                sp.dma_start(priw[:], pri[at(l), :, :].broadcast_to((P, H, ET))).then_inc(s_w, 16)
            WN = 16 * (3 * R4 + 2 * H + 1)

            def wa_load(l):
                for r in range(R4):
                    sp.dma_start(wa[32 * r:32 * r + 32, :, :],
                                 Wa[at(l), :, r:D:R4, :].rearrange("l t i o -> (l i) t o")).then_inc(s_wa, 16)

            def score_(l):
                def body(q, slot, use):
                    hold(sp, s_gath[slot], (l * (QUADS // HALF) + use) * 64 + 64)
                    sp.dma_start(messages[at(q), :, :].rearrange("q p (s c) -> (q p) s c", s=4),
                                 rows[:, slot, :, D:ROW]).then_inc(s_vst[slot], 16)
                quads(sp, body)
                wa_load(l)
                hold(sp, s_wa, l * (16 * R4) + 16 * R4)
                for k in range(HALF):
                    hold(sp, s_vst[k], (l * (QUADS // HALF) + QUADS // HALF) * 16)

            def softmax_(l):
                if isinstance(l, int):
                    return
                weights(l + 1)
                hold(sp, s_w, l * WN + 2 * WN)

            def gatherup_(l):
                def body(q, slot, use):
                    if not is_first(q, HALF):
                        hold(sp, s_wm, l * QUADS + q - (HALF - 1))
                    sp.dma_start(mbuf[:, slot, :], messages[at(q), :, :].rearrange("q p c -> (q p) c")
                                 ).then_inc(s_vld[slot], 16)
                quads(sp, body)

            def project_(l, later):
                def body(t, b, pair):
                    hold(sp, s_tabk, l * TILES + t + 1)
                    hold(sp, s_tabv, l * TILES + t + 1)
                    sp.dma_start(table_tiles[at(t), :, :].rearrange("t p c -> (t p) c"),
                                 tab[:, b].rearrange("p e c -> p (e c)")).then_inc(s_tabst[b], 16)
                tiles(sp, body)
                for b in range(2):
                    n = TILES - TILES // 2 if b == 0 else TILES // 2
                    hold(sp, s_tabst[b], l * (n * 16) + n * 16)

            sp.wait_ge(s_pool0, 3)
            weights(0)
            sp.wait_ge(s_w, WN)
            def last():
                xin = flat[:, 0:TILES * D].rearrange("p (t c) -> p t c", t=TILES)
                sp.dma_start(xin[:, 0:TILES - 1, :],
                             x[0:(TILES - 1) * P, :].rearrange("(t p) c -> p t c", p=P)).then_inc(s_x, 16)
                sp.dma_start(xin[0:LAST, TILES - 1, :], x[(TILES - 1) * P:N, :]).then_inc(s_x, 16)
                sp.wait_ge(s_h, L * TILES + 1)
                sp.dma_start(out[0:(TILES - 1) * P, :].rearrange("(t p) c -> p t c", p=P),
                             h[:, 0:TILES - 1, :]).then_inc(s_out, 16)
                sp.dma_start(out[(TILES - 1) * P:N, :], h[0:LAST, TILES - 1, :]).then_inc(s_out, 16)
                sp.wait_ge(s_out, 32)
            layers(sp, score_, softmax_, gatherup_, lambda l: None, project_, last)

        @block.gpsimd
        def _(pool):
            pool.memset(aT[:].rearrange("p a b c -> p (a b c)")[:, (CB - 1) * P:CB * P].bitcast(I32),
                        int(NO_DST)).then_inc(s_pool0, 1)
            pool.memset(mT[:].rearrange("p a b c -> p (a b c)")[:, (CB - 1) * P:CB * P].bitcast(I32), 0)
            pool.memset(flat[:, (CB - 1) * P:CB * P].bitcast(I32), 0)
            pool.memset(attw[:], 0.0)
            pool.memset(msgw[:], 0.0)
            pool.memset(h[:, TILES - 1, :], 0.0)
            pool.memset(oh[:].rearrange("p a b c -> p (a b c)").bitcast(I32)[:, TILES - 1:TILES], 0)
            pool.drain().then_inc(s_pool0, 2)
            pool.memset(ones[:], 1.0)
            pool.iota(iota_n[:], [[1, P]], base=0, channel_multiplier=0,
                      allow_small_or_imprecise_dtypes=True)
            pool.iota(iota_nb[:], [[1, P]], base=0, channel_multiplier=0,
                      allow_small_or_imprecise_dtypes=True)
            pool.iota(iota_p[:], [[0, 1]], base=0, channel_multiplier=1,
                      allow_small_or_imprecise_dtypes=True)
            pool.iota(score[:].rearrange("p s h -> p (s h)")[:, 0:SP_], [[1, SP_]], base=0,
                      channel_multiplier=0, allow_small_or_imprecise_dtypes=True)
            pool.drain().then_inc(s_pool0, 1)

            def masked(source, t, b):
                pool.tensor_tensor(
                    hm[:, b].rearrange("p t (r i) -> p t r i", r=R4),
                    source.rearrange("p (t i r) -> p t r i", t=1, r=R4).broadcast_to((P, NT, R4, 32)),
                    tmask[:, at(t), :].rearrange("p a (t r i) -> p (a t) r i", r=1, i=1
                                                 ).broadcast_to((P, NT, R4, 32)), ALU.mult)

            def score_(l):
                def body(q, slot, use):
                    if not is_first(q, HALF):
                        hold(pool, s_dot, l * QUADS + q - (HALF - 1))
                        hold(pool, s_vst[slot], (l * (QUADS // HALF) + use) * 16)
                    half = state["half"]
                    if slot == 0:
                        half = state["half"] = 1 - state["half"]
                        pool.tensor_copy(idx_now[:, half, :], idx[:, at(4 * q, 4 * HALF)])
                        pool.drain()
                    for j in range(4):
                        c = 4 * slot + j
                        pool.indirect_dma_start(
                            out=rows[:, slot, j, :], out_offset=None, in_=table,
                            in_offset=bass.IndirectOffsetOnAxis(ap=idx_now[:, half, c:c + 1], axis=0)
                        ).then_inc(s_gath[slot], 16)
                state = {"half": 1}
                quads(pool, body)

            def gatherup_(l):
                def body(q, slot, use):
                    b = slot % 2
                    hold(pool, s_vld[slot], (l * (QUADS // HALF) + use) * 16 + 16)
                    if not is_first(q, 2):
                        hold(pool, s_agg, l * QUADS + q - 1)
                    w = score[:, at(4 * q, 4), :]
                    pool.tensor_tensor(
                        wmsg[:, b, :, 0:D].rearrange("p s (h c) -> p s h c", h=H),
                        mbuf[:, slot, :].rearrange("p (s h c) -> p s h c", s=4, h=H),
                        w.rearrange("p s (h c) -> p s h c", c=1).broadcast_to((P, 4, H, HD)), ALU.mult)
                    pool.tensor_copy(wmsg[:, b, :, D:AW], w)
                    pool.drain().then_inc(s_wm, 1)
                quads(pool, body)

            def output_(l):
                def body(t, b, pair):
                    if is_first(t):
                        hold(pool, s_hn, l * TNS + TNS)
                    if not is_first(t, 2):
                        hold(pool, s_tr, tr_base(l, 1) + t - 1)
                    masked(node[:, at(t), 0:D].rearrange("p a c -> p (a c)"), t, b)
                    pool.drain().then_inc(s_hm, 1)
                tiles(pool, body)

            def project_(l, later):
                def body(t, b, pair):
                    if not is_first(t, 2):
                        hold(pool, s_tr, tr_base(l, 0) + t - 1)
                    masked(h[:, at(t), :].rearrange("p a b -> p (a b)"), t, b)
                    pool.drain().then_inc(s_hm, 1)
                tiles(pool, body)
            layers(pool, score_, lambda l: None, gatherup_, output_, project_)

        @block.tensor
        def _(pe):
            cnt = prod[:, 0, 0:TILES]
            pe.wait_ge(s_pre, 1)
            pe.matmul(ps[0:TILES - 1, 0, 0:1], cnt[:, 1:TILES], ones[:, 0:1], start=True,
                      stop=True).then_inc(s_prepe, 1)
            pe.wait_ge(s_pre, 2)
            below = wmsg[:].rearrange("p a b c -> p (a b c)")[0:TILES - 1, 0:SP_]
            for k in range(2):
                last = pe.matmul(ps[:, k, 0:SP_ // 2], ones[0:TILES - 1, :],
                                 below[:, k * (SP_ // 2):(k + 1) * (SP_ // 2)], start=True, stop=True)
            last.then_inc(s_prepe, 1)
            pe.wait_ge(s_pre, 3)
            for a, (arr, _) in enumerate(prep_arrays()):
                for k in range(2):
                    for kb in range(CB):
                        last = pe.matmul(ps[:, 2 + 2 * a + k, 0:SP_ // 2], arr[:, kb, :],
                                         prep_sel(kb)[:, k * (SP_ // 2):(k + 1) * (SP_ // 2)],
                                         start=(kb == 0), stop=(kb == CB - 1))
            last.then_inc(s_prepe, 1)
            pe.wait_ge(s_pre, 4)
            dsts = prep_dst()
            for e in range(2):
                for k in range(2):
                    last = pe.matmul(ps[0:4, 2 * e + k, 0:SP_ // 2], pick[:, e, :],
                                     dsts[:, k * (SP_ // 2):(k + 1) * (SP_ // 2)], start=True, stop=True)
            last.then_inc(s_prepe, 1)
            for a, v in enumerate((dsts, dloc[:])):
                for kb in range(SB):
                    pe.transpose(psf[:, 2048 + a * 1024 + kb * P:2048 + a * 1024 + (kb + 1) * P],
                                 v[:, kb * P:(kb + 1) * P], ident[:])
            pe.drain().then_inc(s_prepe, 1)

            def turn(l, out_):
                def go(t, b):
                    pe.wait_ge(s_hm, tr_base(l, out_) + t + 1)
                    if not is_first(t, 2):
                        pe.wait_ge(s_hmT, tr_base(l, out_) + t - 1)
                    for t3 in range(NT):
                        last = pe.transpose(ps[:, b, t3 * P:(t3 + 1) * P], hm[:, b, t3, :], ident[:])
                    last.then_inc(s_tr, 1)
                return go

            def project_(l, later):
                go = turn(l, 0)

                def products(t, b):
                    if not is_first(t):
                        pe.wait_ge(s_kvT, l * TILES + t)
                    if not is_first(t, 2):
                        pe.wait_ge(s_tabk, l * TILES + t - 1)
                        pe.wait_ge(s_tabv, l * TILES + t - 1)
                    o = 1 - b
                    for a, w in enumerate((attw, msgw)):
                        for k in range(2):
                            last = pe.matmul(ps[:, 4 + 2 * a + k, 0:3 * D], kvT[:, o, a, :],
                                             w[:, 3 * k:3 * k + 3, :].rearrange("p e c -> p (e c)"),
                                             start=True, stop=True)
                    last.then_inc(s_tabp, 1)

                def body(t, b, pair):
                    if is_first(t):
                        go(0, 0)
                    if not is_last(t, TILES):
                        go(t + 1, 1 - b)
                    pe.wait_ge(s_hmT, tr_base(l, 0) + t + 1)
                    if not is_first(t, 2):
                        pe.wait_ge(s_kvT, l * TILES + t - 1)
                        pe.wait_ge(s_qn, l * TILES + t - 1)
                    for a, w in enumerate((wk, wv)):
                        for t3 in range(NT):
                            pe.matmul(ps[:, 2 + b, a * P:(a + 1) * P], w[:, t3, :], hmT[:, b, t3, :],
                                      start=(t3 == 0), stop=(t3 == NT - 1))
                    for t3 in range(NT):
                        last = pe.matmul(ps[:, 2 + b, 2 * P:3 * P], hmT[:, b, t3, :], wq[:, t3, :],
                                         start=(t3 == 0), stop=(t3 == NT - 1))
                    last.then_inc(s_kvq, 1)
                    if not is_first(t):
                        products(t, b)
                    if is_last(t, TILES):
                        products(t + 1, 1 - b)
                tiles(pe, body)

            def output_(l):
                go = turn(l, 1)

                def body(t, b, pair):
                    if is_first(t):
                        go(0, 0)
                    if not is_last(t, TILES):
                        go(t + 1, 1 - b)
                    pe.wait_ge(s_hmT, tr_base(l, 1) + t + 1)
                    if not is_first(t, 2):
                        pe.wait_ge(s_h, l * TILES + t - 1)
                    for t3 in range(NT):
                        last = pe.matmul(ps[:, 2 + b, 0:D], hmT[:, b, t3, :], wa[:, t3, :],
                                         start=(t3 == 0), stop=(t3 == NT - 1))
                    last.then_inc(s_g, 1)
                tiles(pe, body)

            def score_(l):
                def turn_onehot(q, slot):
                    b = slot % 2
                    pe.wait_ge(s_oh, l * QUADS + q + 1)
                    if not is_first(q, 2):
                        pe.wait_ge(s_ohT, l * QUADS + q - 1)
                    pb = ps[:, b, :].bitcast(BF16)
                    for j in range(4):
                        last = pe.transpose(pb[:, j * P:(j + 1) * P], oh[:, slot % 4, j, :], identb[:])
                    last.then_inc(s_ohp, 1)

                def body(q, slot, use):
                    b = slot % 2
                    if is_first(q):
                        turn_onehot(0, 0)
                    if not is_last(q, QUADS):
                        turn_onehot(q + 1, slot + 1)
                    ts = tiles_of(q, mybir.EngineType.PE)
                    pe.wait_ge(s_ohT, l * QUADS + q + 1)
                    if not is_first(q, 2):
                        pe.wait_ge(s_dot, l * QUADS + q - 1)
                    for j in range(4):
                        last = pe.matmul(ps[:, 2 + b, j * P:(j + 1) * P], ohT[:, b, j, :],
                                         node[:, at(ts[j]), 0:D].rearrange("p a c -> p (a c)"),
                                         start=True, stop=True)
                    last.then_inc(s_qe, 1)
                quads(pe, body)

            def softmax_(l):
                for kb in range(SB):
                    for hh in range(H):
                        last = pe.transpose(ps[:, kb, hh * P:(hh + 1) * P],
                                            score[:, kb * P:(kb + 1) * P, hh], ident[:])
                    last.then_inc(s_smt, 1)
                hold(pe, s_smd, l * SMD + 1)
                for e, lane in enumerate((P - 1, 0)):
                    for kb in range(SB):
                        last = pe.transpose(psf[0:H, e * 1024 + kb * P:e * 1024 + (kb + 1) * P],
                                            mT[:, kb, :, lane], ident[:])
                last.then_inc(s_sml, 1)
                hold(pe, s_smd, l * SMD + 2)
                for e in range(2):
                    for kb in range(SB):
                        last = pe.transpose(ps[:, 4 + e, kb * H:(kb + 1) * H],
                                            carry[:, e, kb * P:(kb + 1) * P], ident[0:H, 0:H])
                last.then_inc(s_smc, 1)
                for kb in range(SB):
                    pe.wait_ge(s_sme, l * SB + (kb + 1))
                    for hh in range(H):
                        last = pe.transpose(ps[:, kb, hh * P:(hh + 1) * P], aT[:, kb, hh, :], ident[:])
                    last.then_inc(s_smb, 1)

            def gatherup_(l):
                def body(q, slot, use):
                    b = slot % 2
                    pe.wait_ge(s_ohf, l * QUADS + q + 1)
                    pe.wait_ge(s_wm, l * QUADS + q + 1)
                    if not is_first(q, 2):
                        pe.wait_ge(s_add, l * QUADS + q - 1)
                    for j in range(4):
                        last = pe.matmul(ps[:, 4 * b + j, 0:AW], ohT[:, b, j, :], wmsg[:, b, j, :],
                                         start=True, stop=True)
                    last.then_inc(s_agg, 1)
                quads(pe, body)
            layers(pe, score_, softmax_, gatherup_, output_, project_)

        @block.scalar
        def _(act):
            def copied(l, out_):
                def body(t, b, pair):
                    act.wait_ge(s_tr, tr_base(l, out_) + t + 1)
                    if not is_first(t, 2):
                        act.wait_ge(s_g if out_ else s_kvq, l * TILES + t - 1)
                    act.copy(hmT[:, b].rearrange("p a c -> p (a c)"), ps[:, b, 0:NT * P]).then_inc(s_hmT, 1)
                return body

            def project_(l, later):
                turned = copied(l, 0)

                def v_half(t, b, pair):
                    act.wait_ge(s_tabp, l * TILES + t + 1)
                    if not is_first(t, 2):
                        act.wait_ge(s_tabst[b], stores_before(l, b, pair))
                    act.copy(tab[:, b, :, D:ROW].rearrange("p (k e) c -> p k e c", k=2),
                             ps[:, 6:8, 0:3 * D].rearrange("p k (e c) -> p k e c", e=3)).then_inc(s_tabv, 1)

                def body(t, b, pair):
                    if is_first(t):
                        turned(0, 0, 0)
                    if not is_last(t, TILES):
                        turned(t + 1, 1 - b, None)
                    act.wait_ge(s_kvq, l * TILES + t + 1)
                    if not is_first(t, 2):
                        act.wait_ge(s_tabp, l * TILES + t - 1)
                    act.copy(kvT[:, b].rearrange("p a c -> p (a c)"), ps[:, 2 + b, 0:2 * P]).then_inc(s_kvT, 1)
                    if not is_first(t):
                        v_half(t - 1, 1 - b, pair - 1 + b)
                    if is_last(t, TILES):
                        v_half(t, b, pair)
                tiles(act, body)

            def score_(l):
                def body(q, slot, use):
                    b = slot % 2
                    act.wait_ge(s_ohp, l * QUADS + q + 1)
                    if not is_first(q, 2):
                        act.wait_ge(s_qe, l * QUADS + q - 1)
                    act.copy(ohT[:, b].rearrange("p s c -> p (s c)"),
                             ps[:, b, :].bitcast(BF16)[:, 0:4 * P]).then_inc(s_ohT, 1)
                quads(act, body)

            def gatherup_(l):
                def body(q, slot, use):
                    b = slot % 2
                    for j in range(4):
                        act.activation(prod[:, b, j * P:(j + 1) * P], iota_n[:], ACT.Square,
                                       bias=dloc[:, at(4 * q + j)], scale=-1.0)
                    act.drain()
                    if not is_first(q, 2):
                        act.wait_ge(s_agg, l * QUADS + q - 1)
                    act.activation(ohT[:, b].rearrange("p s c -> p (s c)"), prod[:, b, :], ACT.Relu,
                                   bias=ones[:, 0:1], scale=-1.0).then_inc(s_ohf, 1)
                quads(act, body)

            def softmax_(l):
                act.wait_ge(s_smd, l * SMD + 3)
                for kb in range(SB):
                    act.activation(aT[:, kb].rearrange("p h c -> p (h c)"),
                                   mT[:, kb].rearrange("p h c -> p (h c)"), ACT.Exp).then_inc(s_sme, 1)
            act.wait_ge(s_load, 16 * 12)
            act.activation(beta[:, :, 0:NT], alpha[:, :, 0:NT], ACT.Exp, scale=-1.0).then_inc(s_act, 1)

            def last():
                act.wait_ge(s_smd, L * SMD + 1)
                act.activation(prod[:, 0, 0:TILES], prod[:, 1, 0:TILES], ACT.Sqrt).then_inc(s_act, 1)
            layers(act, score_, softmax_, gatherup_,
                   lambda l: tiles(act, copied(l, 1)), project_, last)

        @block.vector
        def _(dve):
            f2 = "p a b c -> p (a b c)"
            half = SP_ // 2

            dve.wait_ge(s_pool0, 4)
            dve.tensor_scalar(ident[:], iota_n[:], iota_p[:], None, ALU.is_equal)
            dve.tensor_scalar(identb[:], iota_n[:], iota_p[:], None, ALU.is_equal)
            for e, lane in enumerate((0, P - 1)):
                dve.tensor_scalar(pick[:, e, :], iota_p[:].broadcast_to((P, 4)), float(lane), None, ALU.is_equal)
            dve.wait_ge(s_load, 16 * 12)
            (dstf, _), (idxf, _) = prep_arrays()
            dve.tensor_copy(dstf, aT[:].rearrange(f2)[:, 0:CB * P].bitcast(I32).rearrange("p (k c) -> p k c", k=CB))
            dve.scalar_tensor_tensor(
                out=idxf, in0=mT[:].rearrange(f2)[:, 0:CB * P].bitcast(I32).rearrange("p (k c) -> p k c", k=CB),
                scalar=float(ET), in1=flat[:, 0:CB * P].bitcast(I32).rearrange("p (k c) -> p k c", k=CB),
                op0=ALU.mult, op1=ALU.add)
            dve.drain()
            scratch = wmsg[:].rearrange(f2)[:, 0:CB * P]
            for t in range(1, TILES):
                dve.tensor_scalar(scratch.rearrange("p (k c) -> p k c", k=CB), dstf, float(P * t), None,
                                  ALU.is_lt, ALU.add, accum_out=prod[:, 0, t:t + 1])
                if t < TILES - 1:
                    dve.drain()
            dve.drain().then_inc(s_pre, 1)
            T1 = TILES - 1
            whole = prod[0:T1, 1, 0:1].bitcast(I32)
            rank = prod[0:T1, 1, 1:2]
            iota_s = score[:].rearrange("p s h -> p (s h)")[:, 0:SP_]
            dve.wait_ge(s_prepe, 1)
            dve.tensor_copy(whole, ps[0:T1, 0, 0:1])
            dve.drain()
            dve.tensor_scalar(whole, whole, 7, None, ALU.arith_shift_right)
            dve.drain()
            dve.tensor_scalar(rank, whole, float(CHUNKS - 1), None, ALU.min)
            dve.drain()
            dve.tensor_tensor(rank, rank, iota_p[0:T1, :], ALU.add)
            dve.drain()
            dve.tensor_scalar(wmsg[:].rearrange(f2)[0:T1, 0:SP_], iota_s[0:T1, :], rank, None, ALU.is_gt)
            dve.drain().then_inc(s_pre, 1)
            def two(v):
                return v.rearrange("p (k c) -> p k c", k=2)
            step_chunk = score[:].rearrange("p s h -> p (s h)")[:, SP_:2 * SP_]
            dve.wait_ge(s_prepe, 2)
            dve.tensor_copy(two(tile_of[:]), ps[0:1, 0:2, 0:half])
            dve.tensor_tensor(two(step_chunk), two(iota_s), ps[:, 0:2, 0:half], ALU.subtract)
            dve.drain()
            for kb in range(CB):
                dve.tensor_scalar(prep_sel(kb), step_chunk, float(-P * kb), iota_p[:], ALU.add, ALU.is_equal)
            dve.drain().then_inc(s_pre, 1)
            dve.wait_ge(s_prepe, 3)
            dve.tensor_copy(two(prep_dst()), ps[:, 2:4, 0:half])
            dve.tensor_copy(two(idx[:]), ps[:, 4:6, 0:half])
            dve.drain()
            dve.scalar_tensor_tensor(out=two(dloc[:]), in0=ps[:, 0:2, 0:half], scalar=float(-P),
                                     in1=two(prep_dst()), op0=ALU.mult, op1=ALU.add)
            dve.drain().then_inc(s_pre, 1)

            def to_cap(o, v):
                return dve.tensor_scalar(o, v, 2 * BIG, -BIG, ALU.mult, ALU.add)
            dve.wait_ge(s_prepe, 5)
            first = flat[0:H, 0:SP_]
            last_ = flat[0:H, 1024:1024 + SP_]
            one = flat[0:H, 2048:2048 + SP_]
            same = flat[0:H, 3072:3072 + SP_]
            dve.tensor_copy(two(first), ps[0:H, 0:2, 0:half])
            dve.tensor_copy(two(last_), ps[0:H, 2:4, 0:half])
            dve.memset(join[:], -BIG)
            dve.drain()
            dve.tensor_tensor(one, first, last_, ALU.is_equal)
            dve.tensor_tensor(same[:, 1:SP_], first[:, 1:SP_], last_[:, 0:SP_ - 1], ALU.is_equal)
            dve.drain()
            to_cap(join[:, 1:SP_], same[:, 1:SP_])
            to_cap(one, one)
            dve.drain()
            dve.tensor_tensor(join_fwd[:], one, join[:, 0:SP_], ALU.min)
            dve.tensor_tensor(join_bwd[:], one, join[:, 1:SP_ + 1], ALU.min)
            key = mT[:].rearrange(f2)[:, 0:SP_].rearrange("p (k c) -> p k c", k=SB)
            eq = mT[:].rearrange(f2)[:, SP_:2 * SP_].rearrange("p (k c) -> p k c", k=SB)
            dT = psf[:, 3072:3072 + SP_].rearrange("p (k c) -> p k c", k=SB)
            dve.tensor_copy(key, psf[:, 2048:2048 + SP_].rearrange("p (k c) -> p k c", k=SB))
            dve.memset(seg_cap[:], -BIG)
            dve.drain()
            dve.tensor_tensor(eq[:, :, 1:P], key[:, :, 1:P], key[:, :, 0:P - 1], ALU.is_equal)
            dve.drain()
            caps = seg_cap[:, 0:SB * H * P].rearrange("p (k h c) -> p k h c", k=SB, h=H)
            for hh in range(H):
                to_cap(caps[:, :, hh, 1:P], eq[:, :, 1:P])
            dve.drain()
            dve.tensor_scalar(key, dT, 0.0, None, ALU.is_ge)
            dve.drain()
            dve.scalar_tensor_tensor(out=eq, in0=dT, scalar=float(P - 1), in1=key, op0=ALU.is_le, op1=ALU.mult)
            dve.drain()
            to_cap(lane_cap[:], eq)
            nt_raw = oh[:].rearrange(f2).bitcast(I32)[:, 0:TILES]
            for t3 in range(NT):
                dve.tensor_scalar(tmask[:, :, t3], nt_raw, float(t3), None, ALU.is_equal)
            gate = prod[:, 1, 16:16 + L * NT].rearrange("p (l t) -> p l t", l=L)
            dve.wait_ge(s_act, 1)
            dve.tensor_scalar(gate, beta[:, :, 0:NT], 1.0, None, ALU.add)
            dve.drain()
            dve.reciprocal(gate, gate)
            dve.drain()
            for l in range(L):
                dve.tensor_scalar(alpha[:, l, :], tmask[:, :, 0], gate[:, l, 0:1], None, ALU.mult)
            for t3 in range(1, NT):
                dve.drain()
                for l in range(L):
                    dve.scalar_tensor_tensor(out=alpha[:, l, :], in0=tmask[:, :, t3], scalar=gate[:, l, t3:t3 + 1],
                                             in1=alpha[:, l, :], op0=ALU.mult, op1=ALU.add)
            dve.drain()
            dve.tensor_scalar(beta[:], alpha[:], -1.0, 1.0, ALU.mult, ALU.add)
            dve.memset(score[:, 4 * QUADS:SP_, :], 0.0)

            def project_(l, later):
                dve.tensor_scalar(priw[:], priw[:], float(HD) ** -0.5, None, ALU.mult)
                dve.drain()

                def k_half(t, b, pair):
                    dve.wait_ge(s_tabp, l * TILES + t + 1)
                    if not is_first(t, 2):
                        dve.wait_ge(s_tabst[b], stores_before(l, b, pair))
                    for k in range(2):
                        last = dve.tensor_tensor(
                            tab[:, b, 3 * k:3 * k + 3, 0:D].rearrange("p e (h c) -> p e h c", h=H),
                            ps[:, 4 + k, 0:3 * D].rearrange("p (e h c) -> p e h c", e=3, h=H),
                            priw[:, :, 3 * k:3 * k + 3].rearrange("p h (e c) -> p e h c", c=1
                                                                 ).broadcast_to((P, 3, H, HD)), ALU.mult)
                    last.then_inc(s_tabk, 1)

                def body(t, b, pair):
                    dve.wait_ge(s_kvq, l * TILES + t + 1)
                    dve.wait_ge(s_kvT, l * TILES + t + 1)
                    dve.tensor_copy(node[:, at(t), 0:D].rearrange("p a c -> p (a c)"),
                                    ps[:, 2 + b, 2 * P:3 * P]).then_inc(s_qn, 1)
                    if not is_first(t):
                        k_half(t - 1, 1 - b, pair - 1 + b)
                    if is_last(t, TILES):
                        k_half(t, b, pair)
                tiles(dve, body)

            def output_(l):
                dve.tensor_scalar(rden, node[:, :, D:AW], 0.5, None, ALU.max)
                dve.drain()
                dve.reciprocal(rden, rden)
                dve.drain()
                for a in range(0, TILES, TN):
                    z = min(a + TN, TILES)
                    rows_ = node[:, a:z, 0:D].rearrange("p t (h c) -> p t h c", h=H)
                    dve.tensor_tensor(rows_, rows_,
                                      rden[:, a:z, :].rearrange("p t (h c) -> p t h c", c=1
                                                                ).broadcast_to((P, z - a, H, HD)),
                                      ALU.mult).then_inc(s_hn, 1)
                dve.tensor_tensor(h[:], h[:], beta[:, at(l), :].rearrange("p a (t c) -> p (a t) c", c=1
                                                                          ).broadcast_to((P, TILES, D)), ALU.mult)
                dve.drain()

                def body(t, b, pair):
                    hrow = h[:, at(t), :].rearrange("p a c -> p (a c)")
                    dve.wait_ge(s_g, l * TILES + t + 1)
                    dve.scalar_tensor_tensor(out=hrow, in0=ps[:, 2 + b, 0:D],
                                             scalar=alpha[:, at(l), at(t)].rearrange("p a b -> p (a b)"),
                                             in1=hrow, op0=ALU.mult, op1=ALU.add).then_inc(s_h, 1)
                tiles(dve, body)

            def onehot(out_, q, b):
                for j in range(4):
                    last = dve.tensor_scalar(out_[:, b, j, :], iota_nb[:], dloc[:, at(4 * q + j)], None, ALU.is_equal)
                return last

            def score_(l):
                def body(q, slot, use):
                    b = slot % 2
                    if is_first(q):
                        onehot(oh, 0, 0).then_inc(s_oh, 1)
                        onehot(oh, 1, 1).then_inc(s_oh, 1)
                    if not is_last(q, QUADS) and not is_last(q + 1, QUADS):
                        if not is_first(q, 2):
                            dve.wait_ge(s_ohp, l * QUADS + q - 1)
                        onehot(oh, q + 2, (slot + 2) % 4).then_inc(s_oh, 1)
                    dve.wait_ge(s_qe, l * QUADS + q + 1)
                    dve.wait_ge(s_gath[slot], (l * (QUADS // HALF) + use) * 64 + 64)
                    dve.tensor_tensor(prod[:, b, :].rearrange("p (s c) -> p s c", s=4),
                                      ps[:, 2 + b, :].rearrange("p (s c) -> p s c", s=4),
                                      rows[:, slot, :, 0:D], ALU.mult)
                    dve.drain()
                    dve.tensor_reduce(score[:, at(4 * q, 4), :],
                                      prod[:, b, :].rearrange("p (s h c) -> p s h c", s=4, h=H),
                                      AX, ALU.add).then_inc(s_dot, 1)
                quads(dve, body)

            def softmax_(l):
                n = SB * H * P
                af, mf = aT[:].rearrange(f2), mT[:].rearrange(f2)

                def forward(v):
                    dve.tensor_tensor_scan(mf, seg_cap[:, 0:n], v, -BIG, ALU.min, ALU.max)
                    dve.drain()

                def backward():
                    dve.tensor_tensor_scan(mf[:, ::-1], seg_cap[:, 1:n + 1][:, ::-1], mf[:, ::-1], -BIG,
                                           ALU.min, ALU.max)
                for kb in range(SB):
                    dve.wait_ge(s_smt, l * SB + (kb + 1))
                    dve.tensor_tensor(aT[:, kb], ps[:, kb, :].rearrange("p (h c) -> p h c", h=H),
                                      lane_cap[:, kb, :].rearrange("p (h c) -> p h c", h=1).broadcast_to((P, H, P)),
                                      ALU.min)
                dve.drain()
                forward(af)
                backward()
                dve.drain().then_inc(s_smd, 1)
                dve.memset(run_f[:, 0:1], -BIG)
                dve.memset(run_b[:, SP_:SP_ + 1], -BIG)
                dve.wait_ge(s_sml, l + 1)
                dve.tensor_tensor_scan(run_f[:, 1:SP_ + 1], join_fwd[:], psf[0:H, 0:SP_], -BIG, ALU.min, ALU.max)
                dve.tensor_tensor_scan(run_b[:, 0:SP_][:, ::-1], join_bwd[:, ::-1],
                                       psf[0:H, 1024:1024 + SP_][:, ::-1], -BIG, ALU.min, ALU.max)
                dve.drain()
                dve.tensor_tensor(carry[:, 0, :], run_f[:, 0:SP_], join[:, 0:SP_], ALU.min)
                dve.tensor_tensor(carry[:, 1, :], run_b[:, 1:SP_ + 1], join[:, 1:SP_ + 1], ALU.min)
                dve.drain().then_inc(s_smd, 1)
                dve.wait_ge(s_smc, l + 1)
                for e, lane in enumerate((0, P - 1)):
                    dve.tensor_tensor(mT[:, :, :, lane], mT[:, :, :, lane],
                                      ps[:, 4 + e, 0:SB * H].rearrange("p (k h) -> p k h", k=SB), ALU.max)
                dve.drain()
                forward(mf)
                backward()
                dve.drain()
                dve.tensor_tensor(mf, af, mf, ALU.subtract)
                dve.drain().then_inc(s_smd, 1)
                dve.memset(node[:], 0.0)
                for kb in range(SB):
                    dve.wait_ge(s_smb, l * SB + (kb + 1))
                    dve.tensor_copy(score[:, kb * P:(kb + 1) * P, :].rearrange("p s h -> p h s"),
                                    ps[:, kb, :].rearrange("p (h s) -> p h s", h=H))

            def gatherup_(l):
                def body(q, slot, use):
                    b = slot % 2
                    ts = tiles_of(q, mybir.EngineType.DVE)
                    dve.wait_ge(s_agg, l * QUADS + q + 1)
                    for j in range(4):
                        acc = node[:, at(ts[j]), :].rearrange("p a c -> p (a c)")
                        dve.tensor_tensor(acc, acc, ps[:, 4 * b + j, 0:AW], ALU.add)
                        if j < 3:
                            dve.drain()
                    dve.drain().then_inc(s_add, 1)
                quads(dve, body)

            def last():
                xin = flat[:, 0:TILES * D].rearrange("p (t c) -> p t c", t=TILES)
                stat = prod[:, 1, 0:TILES]
                bc = stat.rearrange("p (t c) -> p t c", c=1).broadcast_to((P, TILES, D))
                dve.wait_ge(s_x, 64)
                dve.tensor_tensor(h[:, 0:TILES - 1, :], h[:, 0:TILES - 1, :], xin[:, 0:TILES - 1, :], ALU.add)
                dve.tensor_tensor(h[0:LAST, TILES - 1, :], h[0:LAST, TILES - 1, :], xin[0:LAST, TILES - 1, :], ALU.add)
                dve.drain()
                dve.tensor_reduce(stat, h[:], AX, ALU.add)
                dve.drain()
                dve.tensor_scalar(stat, stat, 1.0 / D, None, ALU.mult)
                dve.drain()
                dve.tensor_tensor(h[:], h[:], bc, ALU.subtract)
                dve.drain()
                dve.tensor_tensor(node[:, :, 0:D], h[:], h[:], ALU.mult)
                dve.drain()
                dve.tensor_reduce(stat, node[:, :, 0:D], AX, ALU.add)
                dve.drain()
                dve.tensor_scalar(stat, stat, 1.0 / D, EPS, ALU.mult, ALU.add)
                dve.drain().then_inc(s_smd, 1)
                dve.wait_ge(s_act, 2)
                dve.reciprocal(stat, prod[:, 0, 0:TILES])
                dve.drain()
                dve.tensor_tensor(h[:], h[:], bc, ALU.mult)
                dve.drain().then_inc(s_h, 1)
            layers(dve, score_, softmax_, gatherup_, output_, project_, last)


_INS = ['x', 'src', 'dst', 'edge_type_6', 'node_type_3', 'L0_gnn_Wk', 'L0_gnn_Wq', 'L0_gnn_Wv', 'L0_gnn_Wa',
        'L0_gnn_rel_pri', 'L0_gnn_rel_att', 'L0_gnn_rel_msg', 'L0_gnn_skip']


def kernel(**inputs):
    import numpy as _np
    import concourse.bacc as _bacc
    from concourse import mybir as _mybir
    from concourse.bass_utils import run_bass_kernel_spmd as _run

    nc = _bacc.Bacc("TRN2", target_bir_lowering=False, num_devices=1)
    arrays, args = {}, []
    for name in _INS:
        a = _np.ascontiguousarray(inputs[name])
        arrays[f"in_{name}"] = a
        args.append(nc.dram_tensor(f"in_{name}", a.shape, _mybir.dt.from_np(a.dtype), kind="ExternalInput").ap())
    args.append(nc.dram_tensor("out_0", (N, D), _mybir.dt.float32, kind="ExternalOutput").ap())
    gnn(nc, *args)
    r = _run(nc, [arrays], core_ids=[0])
    return r.results[0]["out_0"]
```

```python
from contextlib import ExitStack

import concourse.bass as bass
from concourse import mybir

F32 = mybir.dt.float32
BF16 = mybir.dt.bfloat16
I32 = mybir.dt.int32
ALU = mybir.AluOpType
ACT = mybir.ActivationFunctionType
AX = mybir.AxisListType.X

P = 128
N, E, D, H, HD = 6250, 100000, 128, 4, 32
NT, ET, L = 3, 6, 5
TILES = -(-N // P)
LAST = N - (TILES - 1) * P
CHUNKS = -(-E // P)
CB = -(-CHUNKS // P)
STEPS = CHUNKS + TILES - 1
QUADS = -(-STEPS // 4)
SP_ = 4 * QUADS
BS, BQ = 32, 8
BLOCKS = QUADS // BQ
assert BLOCKS * BQ == QUADS and BS * H == P and BS == 4 * BQ
RING = 2 * BQ
LAG = BQ + 4
ITERS = (QUADS - 2 * RING) // RING
assert QUADS == 2 * RING + ITERS * RING
TU = 8
TN = 13
TNS = -(-TILES // TN)
assert TN >= 8
TITERS = (TILES - 1 - 2 * TU) // TU
assert TILES == 2 * TU + TITERS * TU + 1
ROW = 2 * D
AW = D + H
BIG = 1.5e38
NO_DST = 30000.0
EPS = 1e-5
R4 = D // 32


def gnn(nc, x, src, dst, etype, ntype, Wk, Wq, Wv, Wa, pri, att, msg, skip, out):
    table = nc.dram_tensor("table", (TILES * P * ET, ROW), F32, kind="Internal").ap()
    table_tiles = table.rearrange("(t p e) c -> t p (e c)", p=P, e=ET)

    with ExitStack() as ctx:
        def sb(name, shape, dt=F32):
            return ctx.enter_context(nc.sbuf_tensor(name, shape, dt))

        def sem(name):
            return ctx.enter_context(nc.semaphore(name))

        ps = ctx.enter_context(nc.psum_tensor("ps", [P, 8, 512], F32))
        psf = ps[:].rearrange("p b c -> p (b c)")

        ident = sb("ident", [P, P])
        identb = sb("identb", [P, P], BF16)
        iota_n = sb("iota_n", [P, P])
        iota_nb = sb("iota_nb", [P, P], BF16)
        iota_p = sb("iota_p", [P, 1])
        ones = sb("ones", [P, P])
        pick = sb("pick", [P, 2, 4])
        idx = sb("idx", [P, SP_], I32)
        dloc = sb("dloc", [P, SP_])
        tile_of = sb("tile_of", [1, SP_], I32)
        idx_now = sb("idx_now", [P, 2, BS], I32)
        seg_cap = sb("seg_cap", [P, BLOCKS, P + 1], BF16)
        lane_cap = sb("lane_cap", [P, BLOCKS, P], BF16)
        join = sb("join", [H, SP_ + 1], BF16)
        join_fwd = sb("join_fwd", [H, BLOCKS, BS + 1], BF16)
        join_bwd = sb("join_bwd", [H, SP_], BF16)
        same_step = sb("same_step", [P, BS])
        same_head = sb("same_head", [P, H])
        same_headT = sb("same_headT", [H, P])
        cap4 = sb("cap4", [H, H])
        meets = sb("meets", [P, 2, BLOCKS])
        tmask = sb("tmask", [P, TILES, NT])
        alpha = sb("alpha", [P, L, TILES])
        beta = sb("beta", [P, L, TILES])
        zeros = sb("zeros", [P, AW], BF16)
        wk = sb("wk", [P, NT, D])
        wq = sb("wq", [P, NT, D])
        wv = sb("wv", [P, NT, D])
        wa = sb("wa", [P, NT, D])
        attw = sb("attw", [P, ET, D])
        msgw = sb("msgw", [P, ET, D])
        priw = sb("priw", [P, H, ET])
        h = sb("h", [P, TILES, D])
        qn = sb("qn", [P, TILES, D])
        acc_ = sb("acc", [P, TILES + 1, AW])
        acc = acc_[:, 0:TILES, :]
        rows = sb("rows", [P, RING, 4, ROW])
        oh = sb("oh", [P, 2, 4, P], BF16)
        ohT = sb("ohT", [P, 2, 4, P])
        ohf = sb("ohf", [P, 2, 4, P])
        prod = sb("prod", [P, 2, 4 * D])
        wmsg = sb("wmsg", [P, 2, 4, AW])
        score = sb("score", [P, 2, P])
        weight = sb("weight", [P, 2, P])
        aT = sb("aT", [P, P])
        mT = sb("mT", [P, P])
        seg_now = sb("seg_now", [P, P + 1], BF16)
        join_now = sb("join_now", [H, BS], BF16)
        ends = sb("ends", [P, 2, BS])
        carried = sb("carried", [P, 2])
        last_max = sb("last_max", [H, BS + 1])
        run_f = sb("run_f", [H, BS + 1])
        run_b = sb("run_b", [H, BS + 1])
        carry = sb("carry", [H, 2, BS])
        fade4 = sb("fade4", [H, 2, H])
        fade = sb("fade", [P, H])

        flat = rows[:].rearrange("p a b c -> p (a b c)")
        off = [0]

        def carve(*shape):
            n = 1
            for v in shape:
                n *= v
            v = flat[:, off[0]:off[0] + n]
            off[0] += n
            assert off[0] <= RING * 4 * ROW
            return v
        tab = carve(2, ET * ROW).rearrange("p (b e c) -> p b e c", b=2, e=ET)
        hm = carve(2, NT * D).rearrange("p (b t c) -> p b t c", b=2, t=NT)
        hmT = carve(2, NT * D).rearrange("p (b t c) -> p b t c", b=2, t=NT)
        kvT = carve(2, 2 * D).rearrange("p (b t c) -> p b t c", b=2, t=2)
        rden = carve(TILES, H).rearrange("p (t c) -> p t c", c=H)
        s_load = sem("graph_loaded")
        s_x = sem("x_loaded")
        s_pool0 = sem("constants_ready")
        s_pre = sem("prepare_dve")
        s_prepe = sem("prepare_pe")
        s_w = sem("weights_loaded")
        s_wa = sem("wa_loaded")
        s_phase = sem("phase_ends")
        s_held = sem("waits_held")
        s_hm = sem("masked_ready")
        s_tr = sem("transposed")
        s_hmT = sem("masked_transposed")
        s_kvq = sem("kvq_done")
        s_kvT = sem("kv_copied")
        s_qn = sem("q_copied")
        s_tabp = sem("table_products")
        s_tabk = sem("table_k_half")
        s_tabv = sem("table_v_half")
        s_tabst = [sem(f"table_stored{i}") for i in range(2)]
        s_hn = sem("normalised")
        s_g = sem("wa_product")
        s_h = sem("h_updated")
        s_gath = [sem(f"gathered{i}") for i in range(RING)]
        s_oh = [sem(f"onehot_ready{i}") for i in range(2)]
        s_ohp = sem("onehot_transposed")
        s_ohT = sem("onehot_copied")
        s_qe = sem("q_expanded")
        s_dot = sem("dots_done")
        s_wm = sem("weighted_ready")
        s_ohf = sem("onehot32_ready")
        s_agg = sem("summed")
        s_add = sem("accumulated")
        s_smp = sem("softmax_products")
        s_smd = sem("softmax_dve")
        s_sme = sem("exp_done")
        s_act = sem("gates_and_roots")
        s_out = sem("out_stored")

        def positions(eng, body):
            for k in range(RING):
                body(k, k, 0, k // BQ)
            with eng.Fori(0, ITERS) as it:
                for k in range(RING):
                    body(it * RING + (RING + k), k, it + 1, it * 2 + (2 + k // BQ))
            for q in range(QUADS - RING, QUADS + LAG + 1):
                body(q, q % RING, q // RING, q // BQ)

        def tiles(eng, body):
            for k in range(TU):
                body(k, k % 2, k // 2)
            with eng.Fori(0, TITERS) as it:
                for k in range(TU):
                    body(it * TU + (TU + k), k % 2, it * (TU // 2) + (TU + k) // 2)
            for k in range(TILES - TU - 1, TILES):
                body(k, k % 2, k // 2)

        def stores_before(l, b, pair):
            return (l * (TILES - TILES // 2 if b == 0 else TILES // 2) + pair) * 16

        def at(i, n=1):
            return bass.ds(i, n)

        def tiles_of(q, engine):
            _, ts = nc.values_load_multi_w_load_instructions(
                tile_of[0:1, at(4 * q, 4)], engines=[engine], min_val=0, max_val=TILES - 1,
                skip_runtime_bounds_check_because="a step's tile counts the tiles 1..TILES-1 that began before it")
            return ts

        def is_first(v, n=1):
            return isinstance(v, int) and v < n

        def beyond(v, total=QUADS):
            return isinstance(v, int) and v >= total

        def summed(q):
            a = q - LAG
            return None if is_first(a, 0) or beyond(a) else a

        def piece(slot, n):
            k = slot % BQ
            return (None, None) if k > 3 or is_first(n) or beyond(n - 1, BLOCKS) else (k, n - 1)

        def is_last(v, total):
            return isinstance(v, int) and v == total - 1

        def hold(eng, semaphore, value):
            eng.wait_ge(semaphore, value)
            eng.sem_inc(s_held, 1)

        def end_phase(eng, number):
            eng.drain().then_inc(s_phase, 1)
            hold(eng, s_phase, 5 * number)

        PER = 3

        def number(l, k):
            return 2 + l * PER + k

        def layers(eng, edges_, output_, project_, last=None):
            end_phase(eng, 1)
            project_(0, 0)
            end_phase(eng, 2)

            def one(l):
                edges_(l)
                end_phase(eng, number(l, 1))
                output_(l)
                end_phase(eng, number(l, 2))
            with eng.Fori(0, L - 1) as l:
                one(l)
                project_(l + 1, 1)
                end_phase(eng, number(l, 3))
            one(L - 1)
            if last:
                last()

        def tr_base(l, out_):
            return l * (2 * TILES) + (TILES if out_ else 0)

        SM = 4

        raw_dst = flat[:, 8192:8192 + CB * P]
        dst_f = flat[:, 8192 + CB * P:8192 + 2 * CB * P]
        step_dst = flat[:, 8192 + 2 * CB * P:8192 + 2 * CB * P + SP_]
        raw_src = flat[:, 11264:11264 + CB * P]
        idx_f = flat[:, 11264 + CB * P:11264 + 2 * CB * P]
        iota_s = flat[:, 13312:13312 + SP_]
        step_chunk = flat[:, 13312 + SP_:13312 + 2 * SP_]

        def prep_arrays():
            return ((dst_f.rearrange("p (k c) -> p k c", k=CB), 0),
                    (idx_f.rearrange("p (k c) -> p k c", k=CB), 1))

        def prep_sel(kb):
            return flat[:, 1024 + kb * SP_:1024 + (kb + 1) * SP_]

        def prep_dst():
            return step_dst

        block = ctx.enter_context(nc.Block())

        @block.sync
        def _(sp):
            full = (E // P) // P
            rest = E // P - full * P
            tail = E - (E // P) * P
            for a, b in ((dst, 0), (src, 1), (etype, 2)):
                v = (raw_dst, raw_src, flat[:, 0:CB * P])[b]
                v = v.bitcast(I32).rearrange("p (k c) -> p k c", k=CB)
                sp.wait_ge(s_pool0, 3)
                sp.dma_start(v[:, 0:full, :], a[0:full * P * P].rearrange("(k p c) -> p k c", p=P, c=P)
                             ).then_inc(s_load, 16)
                sp.dma_start(v[0:rest, full, :],
                             a[full * P * P:(full * P + rest) * P].rearrange("(p c) -> p c", c=P)
                             ).then_inc(s_load, 16)
                sp.dma_start(v[rest:rest + 1, full, 0:tail],
                             a[E - tail:E].rearrange("(p c) -> p c", p=1)).then_inc(s_load, 16)
            nt_raw = oh[:].rearrange("p a b c -> p (a b c)").bitcast(I32)[:, 0:TILES]
            sp.dma_start(nt_raw[:, 0:TILES - 1],
                         ntype[0:(TILES - 1) * P].rearrange("(t p) -> p t", p=P),
                         allow_slow_non_contiguous=True).then_inc(s_load, 16)
            sp.dma_start(nt_raw[0:LAST, TILES - 1:TILES],
                         ntype[(TILES - 1) * P:N].rearrange("(p t) -> p t", t=1)).then_inc(s_load, 16)
            sp.dma_start(alpha[:, :, 0:NT], skip.rearrange("(o l) t -> o l t", o=1).broadcast_to((P, L, NT))
                         ).then_inc(s_load, 16)
            sp.dma_start(h[:, 0:TILES - 1, :], x[0:(TILES - 1) * P, :].rearrange("(t p) c -> p t c", p=P)
                         ).then_inc(s_x, 16)
            sp.dma_start(h[0:LAST, TILES - 1, :], x[(TILES - 1) * P:N, :]).then_inc(s_x, 16)
            sp.wait_ge(s_x, 32)

            def weights(l):
                for w, d in ((wk, Wk), (wq, Wq), (wv, Wv)):
                    for r in range(R4):
                        sp.dma_start(w[32 * r:32 * r + 32, :, :],
                                     d[at(l), :, r:D:R4, :].rearrange("l t i o -> (l i) t o")).then_inc(s_w, 16)
                for w, d in ((attw, att), (msgw, msg)):
                    for hh in range(H):
                        a, b = HD * hh, HD * hh + HD
                        sp.dma_start(w[a:b, :, a:b],
                                     d[at(l), hh, :, :, :].rearrange("l t i o -> (l i) t o")).then_inc(s_w, 16)
                sp.dma_start(priw[:], pri[at(l), :, :].broadcast_to((P, H, ET))).then_inc(s_w, 16)
            WN = 16 * (3 * R4 + 2 * H + 1)

            def wa_load(l):
                for r in range(R4):
                    sp.dma_start(wa[32 * r:32 * r + 32, :, :],
                                 Wa[at(l), :, r:D:R4, :].rearrange("l t i o -> (l i) t o")).then_inc(s_wa, 16)

            def edges_(l):
                wa_load(l)
                hold(sp, s_wa, l * (16 * R4) + 16 * R4)
                if not isinstance(l, int):
                    weights(l + 1)
                    hold(sp, s_w, l * WN + 2 * WN)

            def project_(l, later):
                def body(t, b, pair):
                    hold(sp, s_tabk, l * TILES + t + 1)
                    hold(sp, s_tabv, l * TILES + t + 1)
                    sp.dma_start(table_tiles[at(t), :, :].rearrange("t p c -> (t p) c"),
                                 tab[:, b].rearrange("p e c -> p (e c)")).then_inc(s_tabst[b], 16)
                tiles(sp, body)
                for b in range(2):
                    n = TILES - TILES // 2 if b == 0 else TILES // 2
                    hold(sp, s_tabst[b], l * (n * 16) + n * 16)

            sp.wait_ge(s_pool0, 3)
            weights(0)
            sp.wait_ge(s_w, WN)
            def last():
                xin = flat[:, 0:TILES * D].rearrange("p (t c) -> p t c", t=TILES)
                sp.dma_start(xin[:, 0:TILES - 1, :],
                             x[0:(TILES - 1) * P, :].rearrange("(t p) c -> p t c", p=P)).then_inc(s_x, 16)
                sp.dma_start(xin[0:LAST, TILES - 1, :], x[(TILES - 1) * P:N, :]).then_inc(s_x, 16)
                sp.wait_ge(s_h, L * TILES + 1)
                sp.dma_start(out[0:(TILES - 1) * P, :].rearrange("(t p) c -> p t c", p=P),
                             h[:, 0:TILES - 1, :]).then_inc(s_out, 16)
                sp.dma_start(out[(TILES - 1) * P:N, :], h[0:LAST, TILES - 1, :]).then_inc(s_out, 16)
                sp.wait_ge(s_out, 32)
            layers(sp, edges_, lambda l: None, project_, last)

        @block.gpsimd
        def _(pool):
            pool.memset(raw_dst[:, (CB - 1) * P:CB * P].bitcast(I32),
                        int(NO_DST)).then_inc(s_pool0, 1)
            pool.memset(raw_src[:, (CB - 1) * P:CB * P].bitcast(I32), 0)
            pool.memset(flat[:, (CB - 1) * P:CB * P].bitcast(I32), 0)
            pool.memset(attw[:], 0.0)
            pool.memset(msgw[:], 0.0)
            pool.memset(h[:, TILES - 1, :], 0.0)
            pool.memset(oh[:].rearrange("p a b c -> p (a b c)").bitcast(I32)[:, TILES - 1:TILES], 0)
            pool.drain().then_inc(s_pool0, 2)
            pool.memset(ones[:], 1.0)
            pool.memset(zeros[:], 0.0)
            pool.iota(iota_n[:], [[1, P]], base=0, channel_multiplier=0,
                      allow_small_or_imprecise_dtypes=True)
            pool.iota(iota_nb[:], [[1, P]], base=0, channel_multiplier=0,
                      allow_small_or_imprecise_dtypes=True)
            pool.iota(iota_p[:], [[0, 1]], base=0, channel_multiplier=1,
                      allow_small_or_imprecise_dtypes=True)
            pool.iota(iota_s, [[1, SP_]], base=0,
                      channel_multiplier=0, allow_small_or_imprecise_dtypes=True)
            pool.drain().then_inc(s_pool0, 1)

            def masked(source, t, b):
                pool.tensor_tensor(
                    hm[:, b].rearrange("p t (r i) -> p t r i", r=R4),
                    source.rearrange("p (t i r) -> p t r i", t=1, r=R4).broadcast_to((P, NT, R4, 32)),
                    tmask[:, at(t), :].rearrange("p a (t r i) -> p (a t) r i", r=1, i=1
                                                 ).broadcast_to((P, NT, R4, 32)), ALU.mult)

            def edges_(l):
                def body(q, slot, use, n):
                    if beyond(q):
                        return
                    if not is_first(q, RING):
                        hold(pool, s_wm, l * QUADS + q - (RING - 1))
                    half = slot // BQ
                    if slot % BQ == 0:
                        pool.tensor_copy(idx_now[:, half, :], idx[:, at(4 * q, BS)])
                        pool.drain()
                    for j in range(4):
                        c = 4 * (slot % BQ) + j
                        pool.indirect_dma_start(
                            out=rows[:, slot, j, :], out_offset=None, in_=table,
                            in_offset=bass.IndirectOffsetOnAxis(ap=idx_now[:, half, c:c + 1], axis=0)
                        ).then_inc(s_gath[slot], 16)
                positions(pool, body)

            def output_(l):
                def body(t, b, pair):
                    if is_first(t):
                        hold(pool, s_hn, l * TNS + 1)
                    elif not is_first(t, TU) and b == 0:
                        hold(pool, s_hn, l * TNS + TNS)
                    if not is_first(t, 2):
                        hold(pool, s_tr, tr_base(l, 1) + t - 1)
                    masked(acc[:, at(t), 0:D].rearrange("p a c -> p (a c)"), t, b)
                    pool.drain().then_inc(s_hm, 1)
                tiles(pool, body)

            def project_(l, later):
                def body(t, b, pair):
                    if not is_first(t, 2):
                        hold(pool, s_tr, tr_base(l, 0) + t - 1)
                    masked(h[:, at(t), :].rearrange("p a b -> p (a b)"), t, b)
                    pool.drain().then_inc(s_hm, 1)
                tiles(pool, body)
            layers(pool, edges_, output_, project_)

        @block.tensor
        def _(pe):
            cnt = prod[:, 0, 0:TILES]
            pe.wait_ge(s_pre, 1)
            pe.matmul(ps[0:TILES - 1, 0, 0:1], cnt[:, 1:TILES], ones[:, 0:1], start=True,
                      stop=True).then_inc(s_prepe, 1)
            pe.wait_ge(s_pre, 2)
            below = wmsg[:].rearrange("p a b c -> p (a b c)")[0:TILES - 1, 0:SP_]
            for k in range(2):
                last = pe.matmul(ps[:, k, 0:SP_ // 2], ones[0:TILES - 1, :],
                                 below[:, k * (SP_ // 2):(k + 1) * (SP_ // 2)], start=True, stop=True)
            last.then_inc(s_prepe, 1)
            pe.wait_ge(s_pre, 3)
            for a, (arr, _) in enumerate(prep_arrays()):
                for k in range(2):
                    for kb in range(CB):
                        last = pe.matmul(ps[:, 2 + 2 * a + k, 0:SP_ // 2], arr[:, kb, :],
                                         prep_sel(kb)[:, k * (SP_ // 2):(k + 1) * (SP_ // 2)],
                                         start=(kb == 0), stop=(kb == CB - 1))
            last.then_inc(s_prepe, 1)
            pe.wait_ge(s_pre, 4)
            dsts = prep_dst()
            for e in range(2):
                for k in range(2):
                    last = pe.matmul(ps[0:4, 2 * e + k, 0:SP_ // 2], pick[:, e, :],
                                     dsts[:, k * (SP_ // 2):(k + 1) * (SP_ // 2)], start=True, stop=True)
            last.then_inc(s_prepe, 1)
            for a, v in enumerate((acc_, qn)):
                pe.wait_ge(s_pre, 5 + a)
                v = v[:].rearrange("p t c -> p (t c)")
                for n in range(BLOCKS):
                    pe.transpose(psf[:, n * P:(n + 1) * P], v[:, n * P:(n + 1) * P], ident[:])
                if a == 0:
                    pe.matmul(ps[:, 7, 0:BLOCKS], prod[:, 1, P:2 * P], dloc[:, 0:BLOCKS * BS:BS], start=True, stop=True)
                pe.drain().then_inc(s_prepe, 1)

            def turn(l, out_):
                def go(t, b):
                    pe.wait_ge(s_hm, tr_base(l, out_) + t + 1)
                    if not is_first(t, 2):
                        pe.wait_ge(s_hmT, tr_base(l, out_) + t - 1)
                    for t3 in range(NT):
                        last = pe.transpose(ps[:, b, t3 * P:(t3 + 1) * P], hm[:, b, t3, :], ident[:])
                    last.then_inc(s_tr, 1)
                return go

            def project_(l, later):
                go = turn(l, 0)

                def products(t, b):
                    if not is_first(t):
                        pe.wait_ge(s_kvT, l * TILES + t)
                    if not is_first(t, 2):
                        pe.wait_ge(s_tabk, l * TILES + t - 1)
                        pe.wait_ge(s_tabv, l * TILES + t - 1)
                    o = 1 - b
                    for a, w in enumerate((attw, msgw)):
                        for k in range(2):
                            last = pe.matmul(ps[:, 4 + 2 * a + k, 0:3 * D], kvT[:, o, a, :],
                                             w[:, 3 * k:3 * k + 3, :].rearrange("p e c -> p (e c)"),
                                             start=True, stop=True)
                    last.then_inc(s_tabp, 1)

                def body(t, b, pair):
                    if is_first(t):
                        go(0, 0)
                    if not is_last(t, TILES):
                        go(t + 1, 1 - b)
                    pe.wait_ge(s_hmT, tr_base(l, 0) + t + 1)
                    if not is_first(t, 2):
                        pe.wait_ge(s_kvT, l * TILES + t - 1)
                        pe.wait_ge(s_qn, l * TILES + t - 1)
                    for a, w in enumerate((wk, wv)):
                        for t3 in range(NT):
                            pe.matmul(ps[:, 2 + b, a * P:(a + 1) * P], w[:, t3, :], hmT[:, b, t3, :],
                                      start=(t3 == 0), stop=(t3 == NT - 1))
                    for t3 in range(NT):
                        last = pe.matmul(ps[:, 2 + b, 2 * P:3 * P], hmT[:, b, t3, :], wq[:, t3, :],
                                         start=(t3 == 0), stop=(t3 == NT - 1))
                    last.then_inc(s_kvq, 1)
                    if not is_first(t):
                        products(t, b)
                    if is_last(t, TILES):
                        products(t + 1, 1 - b)
                tiles(pe, body)

            def output_(l):
                go = turn(l, 1)

                def body(t, b, pair):
                    if is_first(t):
                        go(0, 0)
                    if not is_last(t, TILES):
                        go(t + 1, 1 - b)
                    pe.wait_ge(s_hmT, tr_base(l, 1) + t + 1)
                    if not is_first(t, 2):
                        pe.wait_ge(s_h, l * TILES + t - 1)
                    for t3 in range(NT):
                        last = pe.matmul(ps[:, 2 + b, 0:D], hmT[:, b, t3, :], wa[:, t3, :],
                                         start=(t3 == 0), stop=(t3 == NT - 1))
                    last.then_inc(s_g, 1)
                tiles(pe, body)

            def edges_(l):
                def turn_onehot(q, b, pair):
                    pe.wait_ge(s_oh[b], l * (QUADS // 2) + pair + 1)
                    if not is_first(q):
                        pe.wait_ge(s_ohT, l * QUADS + q)
                    pb = ps[:, 0, :].bitcast(BF16)
                    for j in range(4):
                        last = pe.transpose(pb[:, j * P:(j + 1) * P], oh[:, b, j, :], identb[:])
                    last.then_inc(s_ohp, 1)

                def softmax_piece(k, n, par):
                    g = l * (SM * BLOCKS) + SM * n
                    if k == 0:
                        if not is_first(n):
                            hold(pe, s_smd, g)
                        hold(pe, s_dot, l * QUADS + BQ * n + BQ)
                        pe.transpose(ps[:, 1, 0:P], score[:, par, :], ident[:]).then_inc(s_smp, 1)
                    if k == 1:
                        hold(pe, s_smd, g + 1)
                        pe.matmul(ps[0:H, 1, 0:2 * BS], same_head[:], ends[:].rearrange("p e s -> p (e s)"),
                                  start=True, stop=True).then_inc(s_smp, 1)
                    if k == 2:
                        hold(pe, s_smd, g + 2)
                        pe.matmul(ps[:, 1, 2 * BS:4 * BS], same_headT[:], carry[:].rearrange("p e s -> p (e s)"),
                                  start=True, stop=True).then_inc(s_smp, 1)
                    if k == 3:
                        hold(pe, s_sme, l * BLOCKS + n + 1)
                        pe.transpose(ps[:, 1, P:2 * P], aT[:], ident[:])
                        pe.matmul(ps[:, 1, 2 * P:2 * P + H], ones[0:H, :], fade4[:, 1, :],
                                  start=True, stop=True).then_inc(s_smp, 1)

                def body(q, slot, use, n):
                    b = slot % 2
                    if is_first(q):
                        turn_onehot(0, 0, 0)
                    if not beyond(q + 1):
                        turn_onehot(q + 1, 1 - b, use * (RING // 2) + (slot + 1) // 2)
                    if not beyond(q):
                        ts = tiles_of(q, mybir.EngineType.PE)
                        pe.wait_ge(s_ohT, l * QUADS + q + 1)
                        if not is_first(q, 2):
                            pe.wait_ge(s_dot, l * QUADS + q - 1)
                        for j in range(4):
                            last = pe.matmul(ps[:, 2 + b, j * P:(j + 1) * P], ohT[:, b, j, :],
                                             qn[:, at(ts[j]), :].rearrange("p a c -> p (a c)"),
                                             start=True, stop=True)
                        last.then_inc(s_qe, 1)
                    a = summed(q)
                    if a is not None:
                        ta = tiles_of(a, mybir.EngineType.PE)
                        pe.wait_ge(s_ohf, l * QUADS + a + 1)
                        pe.wait_ge(s_wm, l * QUADS + a + 1)
                        if not is_first(a, 2):
                            pe.wait_ge(s_add, l * QUADS + a - 1)
                        for i in range(2):
                            bank = ps[:, 4 + 2 * b + i, :]
                            pe.matmul(bank[:, AW:2 * AW], identb[:], zeros[:], start=True, stop=True)
                            pe.matmul(bank[:, 0:AW], ohf[:, b, 2 * i, :], wmsg[:, b, 2 * i, :],
                                      start=False, stop=True, skip_group_check=True)
                            on = nc.s_assert_within(
                                ta[2 * i + 1] - ta[2 * i], 0, 1,
                                skip_runtime_bounds_check_because="a step moves on by one tile at most")
                            last = pe.matmul(bank[:, at(on * AW, AW)],
                                             ohf[:, b, 2 * i + 1, :], wmsg[:, b, 2 * i + 1, :],
                                             start=False, stop=True, skip_group_check=True)
                        last.then_inc(s_agg, 1)
                    k, m = piece(slot, n)
                    if k is not None:
                        softmax_piece(k, m, 1 - slot // BQ)
                positions(pe, body)
            layers(pe, edges_, output_, project_)

        @block.scalar
        def _(act):
            def copied(l, out_):
                def body(t, b, pair):
                    act.wait_ge(s_tr, tr_base(l, out_) + t + 1)
                    if not is_first(t, 2):
                        act.wait_ge(s_g if out_ else s_kvq, l * TILES + t - 1)
                    act.copy(hmT[:, b].rearrange("p a c -> p (a c)"), ps[:, b, 0:NT * P]).then_inc(s_hmT, 1)
                return body

            def project_(l, later):
                turned = copied(l, 0)

                def v_half(t, b, pair):
                    act.wait_ge(s_tabp, l * TILES + t + 1)
                    if not is_first(t, 2):
                        act.wait_ge(s_tabst[b], stores_before(l, b, pair))
                    act.copy(tab[:, b, :, D:ROW].rearrange("p (k e) c -> p k e c", k=2),
                             ps[:, 6:8, 0:3 * D].rearrange("p k (e c) -> p k e c", e=3)).then_inc(s_tabv, 1)

                def body(t, b, pair):
                    if is_first(t):
                        turned(0, 0, 0)
                    if not is_last(t, TILES):
                        turned(t + 1, 1 - b, None)
                    act.wait_ge(s_kvq, l * TILES + t + 1)
                    if not is_first(t, 2):
                        act.wait_ge(s_tabp, l * TILES + t - 1)
                    act.copy(kvT[:, b].rearrange("p a c -> p (a c)"), ps[:, 2 + b, 0:2 * P]).then_inc(s_kvT, 1)
                    if not is_first(t):
                        v_half(t - 1, 1 - b, pair - 1 + b)
                    if is_last(t, TILES):
                        v_half(t, b, pair)
                tiles(act, body)

            def edges_(l):
                squares = prod[:, 1, :].bitcast(BF16).rearrange("p (u c) -> p u c", u=2)

                def onehot(out_, q, b, turn, used=None):
                    if isinstance(q, int):
                        act.drain()
                    for j in range(4):
                        act.activation(squares[:, turn % 2, j * P:(j + 1) * P], iota_n[:], ACT.Square,
                                       bias=dloc[:, at(4 * q + j)], scale=-1.0)
                    act.drain()
                    if used is not None:
                        act.wait_ge(s_agg, used)
                    return act.activation(out_[:, b].rearrange("p s c -> p (s c)"), squares[:, turn % 2, :],
                                          ACT.Relu, bias=ones[:, 0:1], scale=-1.0)

                def body(q, slot, use, n):
                    b = slot % 2
                    turn = 3 * (slot // 2)
                    if is_first(q):
                        onehot(oh, 0, 0, 1).then_inc(s_oh[0], 1)
                    if not beyond(q):
                        act.wait_ge(s_ohp, l * QUADS + q + 1)
                        if not is_first(q, 2):
                            act.wait_ge(s_qe, l * QUADS + q - 1)
                        act.copy(ohT[:, b].rearrange("p s c -> p (s c)"),
                                 ps[:, 0, :].bitcast(BF16)[:, 0:4 * P]).then_inc(s_ohT, 1)
                    k, m = piece(slot, n)
                    if k == 3:
                        act.wait_ge(s_smd, l * (SM * BLOCKS) + SM * m + 3)
                        act.activation(fade4[:, 1, :], fade4[:, 0, :], ACT.Exp)
                        act.activation(aT[:], aT[:], ACT.Exp).then_inc(s_sme, 1)
                    if b == 0 and not beyond(q + 2):
                        onehot(oh, q + 2, b, turn).then_inc(s_oh[b], 1)
                    a = summed(q + 1)
                    if a is not None:
                        onehot(ohf, a, 1 - b, turn + 1 + b, None if is_first(a, 2) else l * QUADS + a - 1).then_inc(s_ohf, 1)
                positions(act, body)

            act.wait_ge(s_load, 16 * 12)
            act.activation(beta[:, :, 0:NT], alpha[:, :, 0:NT], ACT.Exp, scale=-1.0).then_inc(s_act, 1)

            def last():
                act.wait_ge(s_smd, L * SM * BLOCKS + 1)
                act.activation(prod[:, 0, 0:TILES], prod[:, 1, 0:TILES], ACT.Sqrt).then_inc(s_act, 1)
            layers(act, edges_, lambda l: tiles(act, copied(l, 1)), project_, last)

        @block.vector
        def _(dve):
            f2 = "p a b c -> p (a b c)"
            half = SP_ // 2

            dve.wait_ge(s_pool0, 4)
            dve.tensor_scalar(ident[:], iota_n[:], iota_p[:], None, ALU.is_equal)
            dve.tensor_scalar(identb[:], iota_n[:], iota_p[:], None, ALU.is_equal)
            for e, lane in enumerate((0, P - 1)):
                dve.tensor_scalar(pick[:, e, :], iota_p[:].broadcast_to((P, 4)), float(lane), None, ALU.is_equal)
            dve.wait_ge(s_load, 16 * 12)
            (dstf, _), (idxf, _) = prep_arrays()
            dve.tensor_copy(dstf, raw_dst.bitcast(I32).rearrange("p (k c) -> p k c", k=CB))
            dve.scalar_tensor_tensor(
                out=idxf, in0=raw_src.bitcast(I32).rearrange("p (k c) -> p k c", k=CB),
                scalar=float(ET), in1=flat[:, 0:CB * P].bitcast(I32).rearrange("p (k c) -> p k c", k=CB),
                op0=ALU.mult, op1=ALU.add)
            dve.drain()
            scratch = wmsg[:].rearrange(f2)[:, 0:CB * P]
            for t in range(1, TILES):
                dve.tensor_scalar(scratch.rearrange("p (k c) -> p k c", k=CB), dstf, float(P * t), None,
                                  ALU.is_lt, ALU.add, accum_out=prod[:, 0, t:t + 1])
                if t < TILES - 1:
                    dve.drain()
            dve.drain().then_inc(s_pre, 1)
            T1 = TILES - 1
            whole = prod[0:T1, 1, 0:1].bitcast(I32)
            rank = prod[0:T1, 1, 1:2]
            dve.wait_ge(s_prepe, 1)
            dve.tensor_copy(whole, ps[0:T1, 0, 0:1])
            dve.drain()
            dve.tensor_scalar(whole, whole, 7, None, ALU.arith_shift_right)
            dve.drain()
            dve.tensor_scalar(rank, whole, float(CHUNKS - 1), None, ALU.min)
            dve.drain()
            dve.tensor_tensor(rank, rank, iota_p[0:T1, :], ALU.add)
            dve.drain()
            dve.tensor_scalar(wmsg[:].rearrange(f2)[0:T1, 0:SP_], iota_s[0:T1, :], rank, None, ALU.is_gt)
            dve.drain().then_inc(s_pre, 1)
            def two(v):
                return v.rearrange("p (k c) -> p k c", k=2)
            dve.wait_ge(s_prepe, 2)
            dve.tensor_copy(two(tile_of[:]), ps[0:1, 0:2, 0:half])
            dve.tensor_tensor(two(step_chunk), two(iota_s), ps[:, 0:2, 0:half], ALU.subtract)
            dve.drain()
            for kb in range(CB):
                dve.tensor_scalar(prep_sel(kb), step_chunk, float(-P * kb), iota_p[:], ALU.add, ALU.is_equal)
            dve.drain().then_inc(s_pre, 1)
            dve.wait_ge(s_prepe, 3)
            dve.tensor_copy(two(prep_dst()), ps[:, 2:4, 0:half])
            dve.tensor_copy(two(idx[:]), ps[:, 4:6, 0:half])
            dve.drain()
            dve.scalar_tensor_tensor(out=two(dloc[:]), in0=ps[:, 0:2, 0:half], scalar=float(-P),
                                     in1=two(prep_dst()), op0=ALU.mult, op1=ALU.add)
            def repeated(v):
                return v[:, 0:4 * QUADS].rearrange("p (s h) -> p s h", h=1).broadcast_to((P, 4 * QUADS, H))
            dstr, dlocr = (v[:].rearrange("p t c -> p (t c)")[:, 0:BLOCKS * P].rearrange("p (s h) -> p s h", h=H)
                           for v in (acc_, qn))
            dve.tensor_scalar(prod[:, 1, P:2 * P], ones[:], ident[:, 0:1], None, ALU.mult)
            dve.tensor_copy(dstr, repeated(prep_dst()))
            dve.drain()
            dve.tensor_copy(dlocr, repeated(dloc[:]))
            dve.drain().then_inc(s_pre, 1)

            def to_cap(o, v):
                return dve.tensor_scalar(o, v, 2 * BIG, -BIG, ALU.mult, ALU.add)
            dve.wait_ge(s_prepe, 4)
            first = flat[0:H, 0:SP_]
            last_ = flat[0:H, 1024:1024 + SP_]
            one = flat[0:H, 2048:2048 + SP_]
            same = flat[0:H, 3072:3072 + SP_]
            dve.tensor_copy(two(first), ps[0:H, 0:2, 0:half])
            dve.tensor_copy(two(last_), ps[0:H, 2:4, 0:half])
            dve.memset(join[:], -BIG)
            dve.memset(join_fwd[:], -BIG)
            dve.drain().then_inc(s_pre, 1)
            dve.tensor_tensor(one, first, last_, ALU.is_equal)
            dve.tensor_tensor(same[:, 1:SP_], first[:, 1:SP_], last_[:, 0:SP_ - 1], ALU.is_equal)
            dve.drain()
            to_cap(join[:, 1:SP_], same[:, 1:SP_])
            to_cap(one, one)
            dve.drain()
            def by_block(v):
                return v[:, 0:4 * QUADS].rearrange("p (n s) -> p n s", s=BS)
            dve.tensor_tensor(join_fwd[:, :, 1:BS + 1], by_block(one), by_block(join), ALU.min)
            dve.tensor_tensor(join_bwd[:], one, join[:, 1:SP_ + 1], ALU.min)
            NB = BLOCKS * P
            key, eq = (flat[:, a:a + NB].rearrange("p (n c) -> p n c", c=P) for a in (4096, 8192))
            in_psum = psf[:, 0:NB].rearrange("p (n c) -> p n c", c=P)
            dve.memset(seg_cap[:], -BIG)
            dve.wait_ge(s_prepe, 5)
            dve.tensor_copy(key, in_psum)
            dve.tensor_scalar(meets[:, 0, :], ps[:, 7, 0:BLOCKS], iota_p[:], None, ALU.is_equal)
            dve.drain().then_inc(s_pre, 1)
            dve.tensor_scalar(meets[:, 1, :], meets[:, 0, :], -1.0, 1.0, ALU.mult, ALU.add)
            dve.tensor_tensor(eq[:, :, 1:P], key[:, :, 1:P], key[:, :, 0:P - 1], ALU.is_equal)
            dve.drain()
            to_cap(seg_cap[:, :, 1:P], eq[:, :, 1:P])
            dve.wait_ge(s_prepe, 6)
            dve.tensor_scalar(key, in_psum, 0.0, None, ALU.is_ge)
            dve.drain()
            dve.scalar_tensor_tensor(out=eq, in0=in_psum, scalar=float(P - 1), in1=key, op0=ALU.is_le, op1=ALU.mult)
            dve.drain()
            to_cap(lane_cap[:], eq)
            by_step = ident[:].rearrange("p (s h) -> p s h", h=H)
            dve.tensor_reduce(same_step[:], by_step, AX, ALU.add)
            dve.tensor_reduce(same_head[:], by_step.rearrange("p s h -> p h s"), AX, ALU.add)
            dve.tensor_copy(same_headT[:].rearrange("p (s h) -> p s h", h=H),
                            ident[0:H, 0:H].rearrange("p (s h) -> p s h", s=1).broadcast_to((H, BS, H)))
            dve.tensor_scalar(cap4[:], ident[0:H, 0:H], BIG, -BIG, ALU.mult, ALU.add)
            dve.memset(last_max[:], -BIG)
            dve.memset(run_b[:], -BIG)
            nt_raw = oh[:].rearrange(f2).bitcast(I32)[:, 0:TILES]
            for t3 in range(NT):
                dve.tensor_scalar(tmask[:, :, t3], nt_raw, float(t3), None, ALU.is_equal)
            gate = prod[:, 1, 16:16 + L * NT].rearrange("p (l t) -> p l t", l=L)
            dve.wait_ge(s_act, 1)
            dve.tensor_scalar(gate, beta[:, :, 0:NT], 1.0, None, ALU.add)
            dve.drain()
            dve.reciprocal(gate, gate)
            dve.drain()
            for l in range(L):
                dve.tensor_scalar(alpha[:, l, :], tmask[:, :, 0], gate[:, l, 0:1], None, ALU.mult)
            for t3 in range(1, NT):
                dve.drain()
                for l in range(L):
                    dve.scalar_tensor_tensor(out=alpha[:, l, :], in0=tmask[:, :, t3], scalar=gate[:, l, t3:t3 + 1],
                                             in1=alpha[:, l, :], op0=ALU.mult, op1=ALU.add)
            dve.drain()
            dve.tensor_scalar(beta[:], alpha[:], -1.0, 1.0, ALU.mult, ALU.add)

            def project_(l, later):
                dve.tensor_scalar(priw[:], priw[:], float(HD) ** -0.5, None, ALU.mult)
                dve.drain()

                def k_half(t, b, pair):
                    dve.wait_ge(s_tabp, l * TILES + t + 1)
                    if not is_first(t, 2):
                        dve.wait_ge(s_tabst[b], stores_before(l, b, pair))
                    for k in range(2):
                        last = dve.tensor_tensor(
                            tab[:, b, 3 * k:3 * k + 3, 0:D].rearrange("p e (h c) -> p e h c", h=H),
                            ps[:, 4 + k, 0:3 * D].rearrange("p (e h c) -> p e h c", e=3, h=H),
                            priw[:, :, 3 * k:3 * k + 3].rearrange("p h (e c) -> p e h c", c=1
                                                                 ).broadcast_to((P, 3, H, HD)), ALU.mult)
                    last.then_inc(s_tabk, 1)

                def body(t, b, pair):
                    dve.wait_ge(s_kvq, l * TILES + t + 1)
                    dve.wait_ge(s_kvT, l * TILES + t + 1)
                    dve.tensor_copy(qn[:, at(t), :].rearrange("p a c -> p (a c)"),
                                    ps[:, 2 + b, 2 * P:3 * P]).then_inc(s_qn, 1)
                    if not is_first(t):
                        k_half(t - 1, 1 - b, pair - 1 + b)
                    if is_last(t, TILES):
                        k_half(t, b, pair)
                tiles(dve, body)

            def output_(l):
                dve.tensor_scalar(rden, acc[:, :, D:AW], 0.5, None, ALU.max)
                dve.drain()
                dve.reciprocal(rden, rden)
                dve.drain()
                for a in range(0, TILES, TN):
                    z = min(a + TN, TILES)
                    rows_ = acc[:, a:z, 0:D].rearrange("p t (h c) -> p t h c", h=H)
                    dve.tensor_tensor(rows_, rows_,
                                      rden[:, a:z, :].rearrange("p t (h c) -> p t h c", c=1
                                                                ).broadcast_to((P, z - a, H, HD)),
                                      ALU.mult).then_inc(s_hn, 1)
                dve.tensor_tensor(h[:], h[:], beta[:, at(l), :].rearrange("p a (t c) -> p (a t) c", c=1
                                                                          ).broadcast_to((P, TILES, D)), ALU.mult)
                dve.drain()

                def body(t, b, pair):
                    hrow = h[:, at(t), :].rearrange("p a c -> p (a c)")
                    dve.wait_ge(s_g, l * TILES + t + 1)
                    dve.scalar_tensor_tensor(out=hrow, in0=ps[:, 2 + b, 0:D],
                                             scalar=alpha[:, at(l), at(t)].rearrange("p a b -> p (a b)"),
                                             in1=hrow, op0=ALU.mult, op1=ALU.add).then_inc(s_h, 1)
                tiles(dve, body)

            def edges_(l):
                def onehot(q, b):
                    for j in range(4):
                        last = dve.tensor_scalar(oh[:, b, j, :], iota_nb[:], dloc[:, at(4 * q + j)], None,
                                                 ALU.is_equal)
                    return last

                def softmax_piece(k, n, par):
                    g = l * (SM * BLOCKS) + SM * n

                    def maxima():
                        dve.tensor_tensor_scan(mT[:], seg_now[:, 0:P], mT[:], -BIG, ALU.min, ALU.max)
                        dve.drain()
                        dve.tensor_tensor_scan(mT[:, ::-1], seg_now[:, 1:P + 1][:, ::-1], mT[:, ::-1], -BIG,
                                               ALU.min, ALU.max)
                        dve.drain()
                    dve.wait_ge(s_smp, g + (k + 1))
                    if k == 0:
                        dve.tensor_copy(seg_now[:], seg_cap[:, at(n), :].rearrange("p a c -> p (a c)"))
                        dve.tensor_copy(join_now[:], join_bwd[:, at(n * BS, BS)])
                        dve.tensor_tensor(aT[:], ps[:, 1, 0:P], lane_cap[:, at(n), :].rearrange("p a c -> p (a c)"),
                                          ALU.min)
                        dve.drain()
                        dve.tensor_tensor_scan(mT[:], seg_now[:, 0:P], aT[:], -BIG, ALU.min, ALU.max)
                        dve.drain()
                        dve.tensor_tensor_scan(mT[:, ::-1], seg_now[:, 1:P + 1][:, ::-1], mT[:, ::-1], -BIG,
                                               ALU.min, ALU.max)
                        dve.drain()
                        for e, lane in enumerate((P - 1, 0)):
                            dve.tensor_scalar(ends[:, e, :], same_step[:], mT[:, lane:lane + 1], None, ALU.mult)
                    if k == 1:
                        dve.tensor_copy(last_max[:, 1:BS + 1], ps[0:H, 1, 0:BS])
                        dve.tensor_tensor_scan(run_b[:, 0:BS][:, ::-1], join_now[:, ::-1],
                                               ps[0:H, 1, BS:2 * BS][:, ::-1], -BIG, ALU.min, ALU.max)
                        dve.drain()
                        dve.tensor_tensor_scan(run_f[:], join_fwd[:, at(n), :].rearrange("p a c -> p (a c)"),
                                               last_max[:], -BIG, ALU.min, ALU.max)
                        dve.drain()
                        dve.tensor_tensor(carry[:, 0, :], run_f[:, 0:BS], join[:, at(n * BS, BS)], ALU.min)
                        dve.tensor_tensor(carry[:, 1, :], run_b[:, 1:BS + 1], join[:, at(n * BS + 1, BS)], ALU.min)
                        dve.tensor_copy(last_max[:, 0:1], run_f[:, BS:BS + 1])
                    if k == 2:
                        picked = prod[:, 0, 0:2 * BS].rearrange("p (e s) -> p e s", e=2)
                        dve.tensor_tensor(picked, ps[:, 1, 2 * BS:4 * BS].rearrange("p (e s) -> p e s", e=2),
                                          same_step[:].rearrange("p (e s) -> p e s", e=1).broadcast_to((P, 2, BS)),
                                          ALU.mult)
                        dve.drain()
                        dve.tensor_reduce(carried[:], picked, AX, ALU.add)
                        dve.drain()
                        for e, lane in enumerate((0, P - 1)):
                            dve.tensor_tensor(mT[:, lane:lane + 1], mT[:, lane:lane + 1], carried[:, e:e + 1], ALU.max)
                        dve.drain()
                        maxima()
                        dve.tensor_tensor(aT[:], aT[:], mT[:], ALU.subtract)
                        dve.tensor_scalar(fade4[:, 0, :], cap4[:], carried[0:H, 0:1], mT[0:H, 0:1],
                                          ALU.add, ALU.subtract)
                    if k == 3:
                        dve.tensor_copy(weight[:, par, :], ps[:, 1, P:2 * P])
                        dve.scalar_tensor_tensor(
                            out=fade[:], in0=ps[:, 1, 2 * P:2 * P + H],
                            scalar=meets[:, 0, at(n)], in1=meets[:, 1, at(n)].broadcast_to((P, H)),
                            op0=ALU.mult, op1=ALU.add)
                    dve.drain().then_inc(s_smd, 1)

                def body(q, slot, use, n):
                    b = slot % 2
                    a = summed(q)
                    if is_first(q):
                        onehot(1, 1).then_inc(s_oh[1], 1)
                        dve.memset(acc_[:], 0.0)
                        dve.drain()
                    if a is not None:
                        aslot = (slot + RING - LAG) % RING
                        w = weight[:, aslot // BQ, (aslot % BQ) * 4 * H:(aslot % BQ + 1) * 4 * H].rearrange(
                            "p (s h) -> p s h", h=H)
                        if not is_first(a, 2):
                            dve.wait_ge(s_agg, l * QUADS + a - 1)
                        dve.tensor_tensor(
                            wmsg[:, b, :, 0:D].rearrange("p s (h c) -> p s h c", h=H),
                            rows[:, aslot, :, D:ROW].rearrange("p s (h c) -> p s h c", h=H),
                            w.rearrange("p s (h c) -> p s h c", c=1).broadcast_to((P, 4, H, HD)), ALU.mult)
                        dve.tensor_copy(wmsg[:, b, :, D:AW], w).then_inc(s_wm, 1)
                    if b == 1 and not beyond(q + 2):
                        dve.wait_ge(s_ohp, l * QUADS + q + 1)
                        onehot(q + 2, b).then_inc(s_oh[b], 1)
                    c = summed(q - 1)
                    if c is not None:
                        ts = tiles_of(c, mybir.EngineType.DVE)

                    def add_window(i):
                        if c is not None:
                            window = acc_[:, at(ts[2 * i], 2), :].rearrange("p a c -> p (a c)")
                            dve.tensor_tensor(window, window, ps[:, 4 + 2 * (1 - b) + i, 0:2 * AW], ALU.add)
                    if not beyond(q):
                        dve.wait_ge(s_qe, l * QUADS + q + 1)
                        dve.wait_ge(s_gath[slot], (l * (QUADS // RING) + use) * 64 + 64)
                        dve.tensor_tensor(prod[:, 0, :].rearrange("p (s c) -> p s c", s=4),
                                          ps[:, 2 + b, :].rearrange("p (s c) -> p s c", s=4),
                                          rows[:, slot, :, 0:D], ALU.mult)
                    if c is not None:
                        dve.wait_ge(s_agg, l * QUADS + c + 1)
                    add_window(0)
                    dve.drain()
                    if not beyond(q):
                        dve.tensor_reduce(score[:, slot // BQ, (slot % BQ) * 4 * H:(slot % BQ + 1) * 4 * H
                                                ].rearrange("p (s h) -> p s h", h=H),
                                          prod[:, 0, :].rearrange("p (s h c) -> p s h c", s=4, h=H),
                                          AX, ALU.add).then_inc(s_dot, 1)
                    add_window(1)
                    if c is None:
                        dve.drain()
                    else:
                        dve.drain().then_inc(s_add, 1)
                    if a is not None and aslot % BQ == 0 and not is_first(a):
                        t0 = tiles_of(a, mybir.EngineType.DVE)[0]
                        msgs = acc[:, at(t0), 0:D].rearrange("p a (h c) -> p (a h) c", h=H)
                        exps = acc[:, at(t0), D:AW].rearrange("p a h -> p (a h)")
                        dve.tensor_tensor(msgs, msgs, fade[:].rearrange("p (h c) -> p h c", c=1
                                                                       ).broadcast_to((P, H, HD)), ALU.mult)
                        dve.tensor_tensor(exps, exps, fade[:], ALU.mult)
                        dve.drain()
                    k, m = piece(slot, n)
                    if k is not None:
                        softmax_piece(k, m, 1 - slot // BQ)
                positions(dve, body)

            def last():
                xin = flat[:, 0:TILES * D].rearrange("p (t c) -> p t c", t=TILES)
                stat = prod[:, 1, 0:TILES]
                bc = stat.rearrange("p (t c) -> p t c", c=1).broadcast_to((P, TILES, D))
                dve.wait_ge(s_x, 64)
                dve.tensor_tensor(h[:, 0:TILES - 1, :], h[:, 0:TILES - 1, :], xin[:, 0:TILES - 1, :], ALU.add)
                dve.tensor_tensor(h[0:LAST, TILES - 1, :], h[0:LAST, TILES - 1, :], xin[0:LAST, TILES - 1, :], ALU.add)
                dve.drain()
                dve.tensor_reduce(stat, h[:], AX, ALU.add)
                dve.drain()
                dve.tensor_scalar(stat, stat, 1.0 / D, None, ALU.mult)
                dve.drain()
                dve.tensor_tensor(h[:], h[:], bc, ALU.subtract)
                dve.drain()
                dve.tensor_tensor(acc[:, :, 0:D], h[:], h[:], ALU.mult)
                dve.drain()
                dve.tensor_reduce(stat, acc[:, :, 0:D], AX, ALU.add)
                dve.drain()
                dve.tensor_scalar(stat, stat, 1.0 / D, EPS, ALU.mult, ALU.add)
                dve.drain().then_inc(s_smd, 1)
                dve.wait_ge(s_act, 2)
                dve.reciprocal(stat, prod[:, 0, 0:TILES])
                dve.drain()
                dve.tensor_tensor(h[:], h[:], bc, ALU.mult)
                dve.drain().then_inc(s_h, 1)
            layers(dve, edges_, output_, project_, last)


_INS = ['x', 'src', 'dst', 'edge_type_6', 'node_type_3', 'L0_gnn_Wk', 'L0_gnn_Wq', 'L0_gnn_Wv', 'L0_gnn_Wa',
        'L0_gnn_rel_pri', 'L0_gnn_rel_att', 'L0_gnn_rel_msg', 'L0_gnn_skip']


def kernel(**inputs):
    import numpy as _np
    import concourse.bacc as _bacc
    from concourse import mybir as _mybir
    from concourse.bass_utils import run_bass_kernel_spmd as _run

    nc = _bacc.Bacc("TRN2", target_bir_lowering=False, num_devices=1)
    arrays, args = {}, []
    for name in _INS:
        a = _np.ascontiguousarray(inputs[name])
        arrays[f"in_{name}"] = a
        args.append(nc.dram_tensor(f"in_{name}", a.shape, _mybir.dt.from_np(a.dtype), kind="ExternalInput").ap())
    args.append(nc.dram_tensor("out_0", (N, D), _mybir.dt.float32, kind="ExternalOutput").ap())
    gnn(nc, *args)
    r = _run(nc, [arrays], core_ids=[0])
    return r.results[0]["out_0"]
```
